# Optimizing a Trainium2 kernel written in Bass

```python
import numpy as np
import jax
import jax.numpy as jnp

def _softmax(x, axis=-1):
    return jax.nn.softmax(x, axis=axis)

def _gelu(x):
    return jax.nn.gelu(x, approximate=True)

def _silu(x):
    return jax.nn.silu(x)

def _sigmoid(x):
    return jax.nn.sigmoid(x)

def _layernorm(x, axis=-1, eps=1e-05):
    m = jnp.mean(x, axis=axis, keepdims=True)
    v = jnp.var(x, axis=axis, keepdims=True)
    return (x - m) / jnp.sqrt(v + eps)

def _scatter_add(tgt, idx, src, axis=0):
    return tgt.at[idx].add(src)

def _segment_sum(src, seg, n):
    return jax.ops.segment_sum(src, seg, n)
kernel_name = 'mk_xattn_ffn_d1_seqx_r8_b2b9db'

def setup_inputs(seed: int=0):
    np.random.seed(seed)
    _w = jnp.asarray

    def _rec_inputs():
        import jax
        import jax.numpy as jnp
        _rk = jax.random.key(seed)
        x = -0.0003929 + 0.9999 * jax.random.normal(jax.random.fold_in(_rk, 1), (8, 128, 512), jnp.float32)
        _lenS = 128 - jax.random.randint(jax.random.fold_in(_rk, 7), (8,), 0, max(1, 128 // 4) + 1, jnp.int32)
        _lenS2 = 128 - jax.random.randint(jax.random.fold_in(_rk, 8), (8,), 0, max(1, 128 // 4) + 1, jnp.int32)
        _ctx_4096P = jax.random.normal(jax.random.fold_in(_rk, 11), (8, 16, 512), jnp.float32)
        _ctx_4096c = jax.random.dirichlet(jax.random.fold_in(_rk, 511), 0.3 * jnp.ones((16,), jnp.float32), (8, 128))
        _ctx_4096t = jnp.einsum('bsk,bkd->bsd', _ctx_4096c, _ctx_4096P)
        _ctx_4096t = _ctx_4096t * jax.lax.rsqrt(jnp.mean(jnp.square(_ctx_4096t)) + 1e-12) * 0.953939
        ctx_4096 = 2.81802e-05 + 1.00001 * (_ctx_4096t + 0.3 * jax.random.normal(jax.random.fold_in(_rk, 611), (8, 128, 512), jnp.float32))
        _validS = jnp.arange(128)[None, :] < _lenS[:, None]
        _validS2 = jnp.arange(128)[None, :] < _lenS2[:, None]
        _causal = jnp.tril(jnp.ones((128, 128), dtype=bool))
        mask_BxSxS2_ff0 = jnp.where(jnp.ones((8, 128, 128), dtype=bool), 0.0, -1000000000.0).astype(jnp.float32)
        return (x, ctx_4096, mask_BxSxS2_ff0)
    x, ctx_4096, mask_BxSxS2_ff0 = _rec_inputs()

    def _L0_xattn_setup():
        import jax, jax.numpy as jnp
        import numpy as np
        BS, SEQ, D_MODEL = (4, 128, 512)
        N_Q_HEADS, N_KV_HEADS, D_K, D_V = (32, 8, 128, 128)
        ROPE_BASE = 10000.0

        def _rotate_half(x):
            x1, x2 = jnp.split(x, 2, axis=-1)
            return jnp.concatenate([-x2, x1], axis=-1)

        def _apply_rope(x, pos0):
            d = x.shape[-1]
            seq = x.shape[2]
            inv_freq = 1.0 / ROPE_BASE ** (jnp.arange(0, d, 2, dtype=jnp.float32) / d)
            pos = (pos0 + jnp.arange(seq)).astype(jnp.float32)
            ang = pos[:, None] * inv_freq[None, :]
            cos = jnp.concatenate([jnp.cos(ang), jnp.cos(ang)], axis=-1)
            sin = jnp.concatenate([jnp.sin(ang), jnp.sin(ang)], axis=-1)
            return x * cos[None, None] + _rotate_half(x) * sin[None, None]
        key = jax.random.key(seed)
        ks = jax.random.split(key, 8)
        w_scale = 0.02
        return {'query': jax.random.normal(ks[0], (BS, SEQ, D_MODEL), dtype=jnp.float32), 'key': jax.random.normal(ks[1], (BS, SEQ, D_MODEL), dtype=jnp.float32), 'value': jax.random.normal(ks[2], (BS, SEQ, D_MODEL), dtype=jnp.float32), 'mask': jnp.zeros((BS, SEQ, SEQ), dtype=jnp.float32), 'wq': jax.random.normal(ks[3], (D_MODEL, N_Q_HEADS * D_K), dtype=jnp.float32) * w_scale, 'wk': jax.random.normal(ks[4], (D_MODEL, N_KV_HEADS * D_K), dtype=jnp.float32) * w_scale, 'wv': jax.random.normal(ks[5], (D_MODEL, N_KV_HEADS * D_V), dtype=jnp.float32) * w_scale, 'wo': jax.random.normal(ks[6], (N_Q_HEADS * D_V, D_MODEL), dtype=jnp.float32) * w_scale, 'curr_seq_pos': 0}
    _L0_xattn_all = _L0_xattn_setup()
    _L0_xattn_in = {k: v for k, v in _L0_xattn_all.items() if k in ('wq', 'wk', 'wv', 'wo')}
    del _L0_xattn_all

    def _L0_ffn_setup():
        import jax, jax.numpy as jnp
        import numpy as np
        GROUP_SIZE = 128

        def dequantize(imatrix, scales, zeros, group_size, out_dtype):
            rs = jnp.repeat(scales, group_size, axis=0)
            rz = jnp.repeat(zeros, group_size, axis=0)
            return ((imatrix.astype(rs.dtype) - rz.astype(rs.dtype)) * rs).astype(out_dtype)
        key = jax.random.key(seed)
        ks = jax.random.split(key, 10)
        H, I, G = (512, 1792, GROUP_SIZE)
        B, S = (4, 256)
        x = jax.random.normal(ks[0], (B, S, H), dtype=jnp.float32)
        gate_w = jax.random.randint(ks[1], (H, I), 0, 16, dtype=jnp.int32)
        gate_z = jax.random.randint(ks[2], (H // G, I), 0, 16, dtype=jnp.int32)
        gate_s = jax.random.uniform(ks[3], (H // G, I), dtype=jnp.float32) * 0.01
        up_w = jax.random.randint(ks[4], (H, I), 0, 16, dtype=jnp.int32)
        up_z = jax.random.randint(ks[5], (H // G, I), 0, 16, dtype=jnp.int32)
        up_s = jax.random.uniform(ks[6], (H // G, I), dtype=jnp.float32) * 0.01
        down_w = jax.random.randint(ks[7], (I, H), 0, 16, dtype=jnp.int32)
        down_z = jax.random.randint(ks[8], (I // G, H), 0, 16, dtype=jnp.int32)
        down_s = jax.random.uniform(ks[9], (I // G, H), dtype=jnp.float32) * 0.01
        return {'x': x, 'gate_w': gate_w, 'gate_z': gate_z, 'gate_s': gate_s, 'up_w': up_w, 'up_z': up_z, 'up_s': up_s, 'down_w': down_w, 'down_z': down_z, 'down_s': down_s}
    _L0_ffn_all = _L0_ffn_setup()
    _L0_ffn_in = {k: v for k, v in _L0_ffn_all.items() if k in ('gate_w', 'gate_z', 'gate_s', 'up_w', 'up_z', 'up_s', 'down_w', 'down_z', 'down_s')}
    del _L0_ffn_all
    return {'x': x, 'ctx_4096': ctx_4096, 'mask_BxSxS2_ff0': mask_BxSxS2_ff0, 'L0_xattn_wq': _L0_xattn_in['wq'], 'L0_xattn_wk': _L0_xattn_in['wk'], 'L0_xattn_wv': _L0_xattn_in['wv'], 'L0_xattn_wo': _L0_xattn_in['wo'], 'L0_ffn_gate_w': _L0_ffn_in['gate_w'], 'L0_ffn_gate_z': _L0_ffn_in['gate_z'], 'L0_ffn_gate_s': _L0_ffn_in['gate_s'], 'L0_ffn_up_w': _L0_ffn_in['up_w'], 'L0_ffn_up_z': _L0_ffn_in['up_z'], 'L0_ffn_up_s': _L0_ffn_in['up_s'], 'L0_ffn_down_w': _L0_ffn_in['down_w'], 'L0_ffn_down_z': _L0_ffn_in['down_z'], 'L0_ffn_down_s': _L0_ffn_in['down_s']}

def reference(x, ctx_4096, mask_BxSxS2_ff0, L0_xattn_wq, L0_xattn_wk, L0_xattn_wv, L0_xattn_wo, L0_ffn_gate_w, L0_ffn_gate_z, L0_ffn_gate_s, L0_ffn_up_w, L0_ffn_up_z, L0_ffn_up_s, L0_ffn_down_w, L0_ffn_down_z, L0_ffn_down_s):
    import jax
    import jax.numpy as jnp

    def _L0_xattn_ref(query, key, value, mask, wq, wk, wv, wo, curr_seq_pos):
        import jax, jax.numpy as jnp
        import numpy as np
        BS, SEQ, D_MODEL = (4, 128, 512)
        N_Q_HEADS, N_KV_HEADS, D_K, D_V = (32, 8, 128, 128)
        ROPE_BASE = 10000.0

        def _rotate_half(x):
            x1, x2 = jnp.split(x, 2, axis=-1)
            return jnp.concatenate([-x2, x1], axis=-1)

        def _apply_rope(x, pos0):
            d = x.shape[-1]
            seq = x.shape[2]
            inv_freq = 1.0 / ROPE_BASE ** (jnp.arange(0, d, 2, dtype=jnp.float32) / d)
            pos = (pos0 + jnp.arange(seq)).astype(jnp.float32)
            ang = pos[:, None] * inv_freq[None, :]
            cos = jnp.concatenate([jnp.cos(ang), jnp.cos(ang)], axis=-1)
            sin = jnp.concatenate([jnp.sin(ang), jnp.sin(ang)], axis=-1)
            return x * cos[None, None] + _rotate_half(x) * sin[None, None]
        bs, sq, _ = query.shape
        n_groups = N_Q_HEADS // N_KV_HEADS
        q = (query @ wq).reshape(bs, sq, N_Q_HEADS, D_K).transpose((0, 2, 1, 3))
        sk = key.shape[1]
        k = (key @ wk).reshape(bs, sk, N_KV_HEADS, 1, D_K)
        k = jnp.repeat(k, n_groups, axis=3).reshape(bs, sk, N_Q_HEADS, D_K).transpose((0, 2, 1, 3))
        v = (value @ wv).reshape(bs, sk, N_KV_HEADS, 1, D_V)
        v = jnp.repeat(v, n_groups, axis=3).reshape(bs, sk, N_Q_HEADS, D_V).transpose((0, 2, 1, 3))
        scale = jnp.sqrt(jnp.float32(D_K))
        q = _apply_rope(q, curr_seq_pos)
        k = _apply_rope(k, curr_seq_pos)
        raw = jnp.einsum('bhqd,bhkd->bhqk', q, k) / scale
        masked = raw + mask[:bs, None, curr_seq_pos:curr_seq_pos + sq, :sk]
        attn = jax.nn.softmax(masked, axis=-1)
        out = jnp.einsum('bhqk,bhkd->bhqd', attn, v)
        out = out.transpose((0, 2, 1, 3)).reshape(bs, sq, N_Q_HEADS * D_V)
        return out @ wo

    def _L0_ffn_ref(x, gate_w, gate_z, gate_s, up_w, up_z, up_s, down_w, down_z, down_s):
        import jax, jax.numpy as jnp
        import numpy as np
        GROUP_SIZE = 128

        def dequantize(imatrix, scales, zeros, group_size, out_dtype):
            rs = jnp.repeat(scales, group_size, axis=0)
            rz = jnp.repeat(zeros, group_size, axis=0)
            return ((imatrix.astype(rs.dtype) - rz.astype(rs.dtype)) * rs).astype(out_dtype)
        dt = x.dtype
        gate_proj = dequantize(gate_w, gate_s, gate_z, GROUP_SIZE, dt)
        up_proj = dequantize(up_w, up_s, up_z, GROUP_SIZE, dt)
        down_proj = dequantize(down_w, down_s, down_z, GROUP_SIZE, dt)
        gate = jax.nn.silu(jnp.dot(x, gate_proj))
        up = jnp.dot(x, up_proj)
        return jnp.dot(gate * up, down_proj)
    x = x + _L0_xattn_ref(_layernorm(x, axis=-1), ctx_4096, ctx_4096, mask_BxSxS2_ff0, L0_xattn_wq, L0_xattn_wk, L0_xattn_wv, L0_xattn_wo, 0)
    x = x + _L0_ffn_ref(_layernorm(x, axis=-1), L0_ffn_gate_w, L0_ffn_gate_z, L0_ffn_gate_s, L0_ffn_up_w, L0_ffn_up_z, L0_ffn_up_s, L0_ffn_down_w, L0_ffn_down_z, L0_ffn_down_s)
    return x

_drawn_inputs = setup_inputs


def setup_inputs(seed=0):
    import zlib

    import numpy as np

    out = dict(_drawn_inputs(seed))
    spreads = {}
    factors = {'L0_xattn_wq': 2.936, 'L0_xattn_wk': 2.962}
    for name, (base, spread) in spreads.items():
        noise = np.random.default_rng([zlib.crc32(name.encode()), seed]).standard_normal(out[name].shape)
        drawn = base * np.exp(spread * noise) if base else spread * noise
        out[name] = jnp.asarray(drawn.astype(out[name].dtype))
    for name, factor in factors.items():
        out[name] = (out[name] * factor).astype(out[name].dtype)
    return out
```

```python
from contextlib import ExitStack

import numpy as np

import concourse.bass as bass
from concourse import mybir

F32 = mybir.dt.float32
F32R = mybir.dt.float32r
I32 = mybir.dt.int32
ALU = mybir.AluOpType
ACT = mybir.ActivationFunctionType
RMAX = bass.bass_isa.ReduceOp.max

P = 128
B = 8
SEQ = 128
DM = 512
KT = DM // P
DK = 128
GROUPS = 8
HPG = 4
HB = B // 2
TOK = HB * SEQ
TILES = GROUPS * B
FF = 1792
FT = FF // (2 * P)
NW = 6
EPS = 1e-5
ROPE_BASE = 10000.0
SCALE = float(DK) ** -0.5

CHUNKS = 6
POS_K, POS_V = 0, 5
HEAD_OF = {1: 0, 2: 1, 3: 2, 4: 3}
CHUNKS_AT = ((0, 1), (2, 3), (4,), (5,))
CONVERT_AT = {1: (0, 1), 2: (2, 3), 3: (4,), 4: (5,)}


def wait_pos(e, sem, value):
    if isinstance(value, int) and value <= 0:
        return
    e.wait_ge(sem, value)


def build(nc, x, ctx, mask, wq, wk, wv, wo, gate_w, gate_z, gate_s, up_w, up_z, up_s,
          down_w, down_z, down_s, cos_in, sin_in, out):
    with ExitStack() as top:
        def sb(stack, name, shape, dt=F32):
            return stack.enter_context(nc.sbuf_tensor(name, shape, dt))

        def sem(name):
            return top.enter_context(nc.semaphore(name))

        acc = sb(top, "acc", [P, B, DM])
        xT_hi = sb(top, "xT_hi", [P, KT, B * SEQ], F32R)
        xT_lo = sb(top, "xT_lo", [P, KT, B * SEQ], F32R)
        Qf = sb(top, "Qf", [P, 2, HB, HPG, SEQ])
        stage = Qf[:, 1].rearrange("p b h q -> p b (h q)")
        cosT = sb(top, "cosT", [P, SEQ])
        sinT = sb(top, "sinT", [P, SEQ])
        ident = sb(top, "ident", [P, P])
        ones = sb(top, "ones", [P, P], F32R)
        ones_f = sb(top, "ones_f", [P, P])
        bn = sb(top, "bn", [P, B, 6])
        mv = sb(top, "mv", [P, B, 2])
        veps = sb(top, "veps", [P, B])
        sd = sb(top, "sd", [P, B])
        rstd = sb(top, "rstd", [P, B])
        nt = sb(top, "nt", [P, B])

        with ExitStack() as a:
            cT_hi = sb(a, "cT_hi", [P, KT, B * SEQ], F32R)
            cT_lo = sb(a, "cT_lo", [P, KT, B * SEQ], F32R)
            W_hi = sb(a, "W_hi", [P, CHUNKS, KT, DK], F32R)
            W_lo = sb(a, "W_lo", [P, CHUNKS, KT, DK], F32R)
            W_raw = sb(a, "W_raw", [P, 2, KT, DK])
            wo_raw = sb(a, "wo_raw", [P, HPG, DM])
            wo_hi = sb(a, "wo_hi", [P, HPG, DM], F32R)
            wo_lo = sb(a, "wo_lo", [P, HPG, DM], F32R)
            Q_hi = sb(a, "Q_hi", [P, 2, HPG * SEQ], F32R)
            Q_lo = sb(a, "Q_lo", [P, 2, HPG * SEQ], F32R)
            K_hi = sb(a, "K_hi", [P, 2, HB, SEQ], F32R)
            K_lo = sb(a, "K_lo", [P, 2, HB, SEQ], F32R)
            V_hi = sb(a, "V_hi", [P, 2, HB, DK], F32R)
            V_lo = sb(a, "V_lo", [P, 2, HB, DK], F32R)
            maskT = sb(a, "maskT", [P, B, SEQ])
            kvf = sb(a, "kvf", [P, TOK])
            rot = sb(a, "rot", [P, 2, TOK])
            sc = sb(a, "sc", [P, 2, HPG * SEQ])
            smax = sb(a, "smax", [P, HPG * SEQ])
            P_hi = sb(a, "P_hi", [P, 2, HPG * SEQ], F32R)
            P_lo = sb(a, "P_lo", [P, 2, HPG * SEQ], F32R)
            seed = sb(a, "seed", [P, HPG * SEQ])
            nrec = sb(a, "nrec", [P, HPG * SEQ])
            O_hi = sb(a, "O_hi", [P, HPG * SEQ], F32R)
            O_lo = sb(a, "O_lo", [P, HPG * SEQ], F32R)
        mask_raw = (seed, nrec)

        with ExitStack() as f:
            F_w = sb(f, "F_w", [P, NW, DM])
            F_z = sb(f, "F_z", [P, NW, DM], I32)
            F_s = sb(f, "F_s", [P, NW, DM])
            G_hi = sb(f, "G_hi", [P, NW, DM], F32R)
            G_lo = sb(f, "G_lo", [P, NW, DM], F32R)
            sg = sb(f, "sg", [P, TOK])
            hf = sb(f, "hf", [P, TOK])
            h_hi = sb(f, "h_hi", [P, 2, B * SEQ], F32R)
            h_lo = sb(f, "h_lo", [P, 2, B * SEQ], F32R)

        ps = top.enter_context(nc.psum_tensor("ps", [P, 8, 512], F32))
        BANK_PROJ, BANK_SC, BANK_PV, BANK_SUM, BANK_OP, BANK_VT = 0, 2, 4, 5, 6, 7
        JOB_BANKS = (2, 3, 4, 5)
        BANK_GATE, BANK_UP, BANK_DOWN = 0, 2, 4

        s_const, s_ident, s_ones_f, s_ones = sem("s_const"), sem("s_ident"), sem("s_ones_f"), sem("s_ones")
        s_rstd = sem("s_rstd")
        s_x = [sem(f"s_x{b}") for b in range(B)]
        s_c = [sem(f"s_c{b}") for b in range(HB)]
        s_m = [sem(f"s_m{b}") for b in range(2)]
        s_chain, s_sqrt, s_xn = sem("s_chain"), sem("s_sqrt"), sem("s_xn")
        s_job, s_job_hi, s_job_lo = sem("s_job"), sem("s_job_hi"), sem("s_job_lo")
        s_raw = [sem("s_raw0"), sem("s_raw1")]
        s_whi, s_wlo = sem("s_whi"), sem("s_wlo")
        s_wo_raw, s_wo_hi, s_wo_lo = sem("s_wo_raw"), sem("s_wo_hi"), sem("s_wo_lo")
        s_proj, s_rot, s_roped = sem("s_proj"), sem("s_rot"), sem("s_roped")
        s_rope_cos, s_rope_sin = sem("s_rope_cos"), sem("s_rope_sin")
        s_khi, s_klo = sem("s_khi"), sem("s_klo")
        s_vcopy, s_vt, s_vhi, s_vlo = sem("s_vcopy"), sem("s_vt"), sem("s_vhi"), sem("s_vlo")
        s_qhi, s_qlo, s_qlo_first = sem("s_qhi"), sem("s_qlo"), sem("s_qlo_first")
        s_scores, s_masked, s_max_go = sem("s_scores"), sem("s_masked"), sem("s_max_go")
        s_max, s_shift = sem("s_max"), sem("s_shift")
        s_exp, s_phi, s_plo = sem("s_exp"), sem("s_phi"), sem("s_plo")
        s_sum, s_pv, s_ln, s_seed = sem("s_sum"), sem("s_pv"), sem("s_ln"), sem("s_seed")
        s_newton, s_on, s_ohi, s_olo = sem("s_newton"), sem("s_on"), sem("s_ohi"), sem("s_olo")
        s_op, s_acc = sem("s_op"), sem("s_acc")
        s_fin = [sem(f"s_fin{m}") for m in range(NW)]
        s_fsub, s_fmul, s_fhi, s_flo = sem("s_fsub"), sem("s_fmul"), sem("s_fhi"), sem("s_flo")
        s_gu, s_silu, s_h, s_hhi, s_hlo = sem("s_gu"), sem("s_silu"), sem("s_h"), sem("s_hhi"), sem("s_hlo")
        s_down, s_facc, s_out = sem("s_down"), sem("s_facc"), sem("s_out")

        JOBS = [("c", b) for b in range(HB)] + [("x", b) for b in range(HB)] + [("m", 0)]
        FIRST_JOBS = len(JOBS)
        JOBS += [("c", b) for b in range(HB, B)] + [("x", b) for b in range(HB, B)] + [("m", 1)]
        ATT_JOBS = len(JOBS)
        JOBS += [("y", b) for b in range(B)]

        def lo_jobs(n):
            return sum(what != "m" for what, _ in JOBS[:n])

        STAGED = [n for n, (what, _) in enumerate(JOBS) if what != "m"]

        def stage_of(n):
            return stage[:, STAGED.index(n) % 4, :]

        def staged_before(n):
            k = STAGED.index(n) - 4
            return STAGED[k] if k >= 0 else None

        def normalised_before(n):
            return sum(what in "xy" for what, _ in JOBS[:n])

        wq_v = wq.rearrange("(t p) n -> p t n", p=P)
        wk_v = wk.rearrange("(t p) n -> p t n", p=P)
        wv_v = wv.rearrange("(t p) n -> p t n", p=P)
        wo_v = wo.rearrange("(h p) n -> p h n", p=DK)
        gate_v = gate_w.rearrange("(t p) n -> p t n", p=P)
        up_v = up_w.rearrange("(t p) n -> p t n", p=P)

        cos_b = cosT[:, :].unsqueeze(1).broadcast_to([P, HB, SEQ])

        sin_b = sinT[:, :].unsqueeze(1).broadcast_to([P, HB, SEQ])

        def by_batch(ap):
            return ap.rearrange("p (b q) -> p b q", b=HB)

        def read_chunk_wait(e, c_unit, pos):
            if pos == POS_V:
                wait_pos(e, s_vcopy, c_unit + 1)
            else:
                wait_pos(e, s_rope_cos, 5 * c_unit + pos + 1)

        block = top.enter_context(nc.Block())

        @block.sync
        def _(sp):
            def load_piece(group, pos):
                wait_pos(sp, s_wlo, CHUNKS * group + pos - 1)
                if pos == POS_K:
                    src = wk_v[:, :, bass.ds(group * DK, DK)]
                elif pos == POS_V:
                    src = wv_v[:, :, bass.ds(group * DK, DK)]
                else:
                    src = wq_v[:, :, bass.ds((group * HPG + HEAD_OF[pos]) * DK, DK)]
                sp.dma_start(W_raw[:, pos % 2], src).then_inc(s_raw[pos % 2], 16)

            def load_wo(group):
                wait_pos(sp, s_wo_lo, HPG * group)
                sp.dma_start(wo_raw[:, :, :], wo_v[:, bass.ds(group * HPG, HPG), :]).then_inc(s_wo_raw, 16)

            for b in range(HB):
                sp.dma_start(stage[:, b, :], ctx[b]).then_inc(s_c[b], 16)
            sp.dma_start(cosT[:, :], cos_in).then_inc(s_const, 16)
            sp.dma_start(sinT[:, :], sin_in).then_inc(s_const, 16)
            for pos in (0, 1):
                load_piece(0, pos)
            for b in range(B):
                sp.dma_start(acc[:, b, :], x[b]).then_inc(s_x[b], 16)
            for half in range(2):
                sp.dma_start(mask_raw[half][:, :].rearrange("p (b k) -> p b k", b=HB),
                             mask[half * HB:(half + 1) * HB].rearrange("b q k -> q b k")).then_inc(s_m[half], 16)
            for pos in range(2, CHUNKS):
                load_piece(0, pos)
            load_wo(0)
            for n in range(FIRST_JOBS, ATT_JOBS):
                what, b = JOBS[n]
                if what == "c":
                    sp.wait_ge(s_job, staged_before(n) + 1)
                    sp.dma_start(stage_of(n), ctx[b]).then_inc(s_c[b - HB], 16)

            with sp.Fori(0, GROUPS - 1) as g:
                for pos in range(CHUNKS):
                    load_piece(g + 1, pos)
                load_wo(g + 1)

            def load_ffn(t, m):
                if m < 4:
                    w_v, z, s = (gate_v, gate_z, gate_s) if m % 2 == 0 else (up_v, up_z, up_s)
                    col = t * (2 * P) + (m // 2) * P
                    sp.dma_start(F_w[:, m, :].bitcast(I32).rearrange("p (t n) -> p t n", t=KT),
                                 w_v[:, :, bass.ds(col, P)]).then_inc(s_fin[m], 16)
                    for dst, src in ((F_z, z), (F_s, s)):
                        sp.dma_start(dst[:, m, :].rearrange("p (t n) -> p t n", t=KT),
                                     src[:, bass.ds(col, P)].partition_broadcast(P)).then_inc(s_fin[m], 16)
                else:
                    row = t * (2 * P) + (m - 4) * P
                    sp.dma_start(F_w[:, m, :].bitcast(I32), down_w[bass.ds(row, P), :]).then_inc(s_fin[m], 16)
                    for dst, src in ((F_z, down_z), (F_s, down_s)):
                        sp.dma_start(dst[:, m:m + 1, :],
                                     src[bass.ds(t * 2 + (m - 4), 1), :].partition_broadcast(P)).then_inc(s_fin[m], 16)

            sp.wait_ge(s_proj, CHUNKS * 2 * GROUPS)
            for m in range(NW):
                load_ffn(0, m)
            with sp.Fori(0, FT - 1) as t:
                for m in range(NW):
                    sp.wait_ge(s_flo, t * NW + m + 1)
                    load_ffn(t + 1, m)
            for half in range(2):
                for b in range(HB):
                    sp.wait_ge(s_facc, B * (FT - 1) + half * HB + b + 1)
                    sp.dma_start(out[half * HB + b], acc[:, half * HB + b, :]).then_inc(s_out, 16)
            sp.wait_ge(s_out, 16 * B)

        @block.gpsimd
        def _(pool):
            nc.gpsimd.memset(ones_f[:, :], 1.0).then_inc(s_ones_f, 1)
            nc.gpsimd.memset(ident[:, :], 0.0).then_inc(s_ident, 1)
            pool.wait_ge(s_ident, 1)
            nc.gpsimd.affine_select(out=ident[:, :], in_=ident[:, :], compare_op=ALU.not_equal, fill=1.0,
                                    base=0, pattern=[[-1, P]], channel_multiplier=1).then_inc(s_ident, 1)

            def split_piece(group, pos):
                pool.wait_ge(s_whi, group * CHUNKS + pos + 1)
                nc.gpsimd.tensor_tensor(W_lo[:, pos], W_raw[:, pos % 2], W_hi[:, pos].bitcast(F32),
                                        ALU.subtract).then_inc(s_wlo, 1)

            def qlo(s, k):
                pool.wait_ge(s_qhi, s + 1)
                nc.gpsimd.tensor_tensor(Q_lo[:, k % 2, :],
                                        Qf[:, (k // HB) % 2, k % HB].rearrange("p h q -> p (h q)"),
                                        Q_hi[:, k % 2, :].bitcast(F32), ALU.subtract).then_inc(s_qlo, 1)

            def tile(g, k, last=False):
                s = g * B + k
                pool.wait_ge(s_masked, s + 1)
                wait_pos(pool, s_shift, s)
                pool.sem_inc(s_max_go, 1)
                nc.gpsimd.partition_all_reduce(smax[:, :], sc[:, k % 2, :], P, RMAX).then_inc(s_max, 1)
                pool.wait_ge(s_max, s + 1)
                nc.gpsimd.tensor_tensor(sc[:, k % 2, :], sc[:, k % 2, :], smax[:, :],
                                        ALU.subtract).then_inc(s_shift, 1)
                if k % HB < 2:
                    qlo(s + 2, k + 2)
                elif k % HB == HB - 1 and not (last and k == B - 1):
                    qlo(s + 2, k + 2)
                if not last:
                    for pos in CONVERT_AT.get(k, ()):
                        split_piece(g + 1, pos)

            for pos in range(CHUNKS):
                split_piece(0, pos)
            qlo(1, 1)
            with pool.Fori(0, GROUPS - 1) as g:
                for k in range(B):
                    tile(g, k)
            for k in range(B):
                tile(GROUPS - 1, k, last=True)

            def scale_piece(t, m):
                pool.wait_ge(s_fsub, t * NW + m + 1)
                nc.gpsimd.tensor_tensor(F_w[:, m, :], F_w[:, m, :], F_s[:, m, :], ALU.mult).then_inc(s_fmul, 1)

            for m in (0, 1):
                scale_piece(0, m)
            with pool.Fori(0, FT - 1) as t:
                for m in (2, 3, 4, 5):
                    scale_piece(t, m)
                for m in (0, 1):
                    scale_piece(t + 1, m)
            for m in (2, 3, 4, 5):
                scale_piece(FT - 1, m)

        @block.scalar
        def _(act):
            def job(n):
                what, b = JOBS[n]
                bank = ps[:, JOB_BANKS[n % 4], :]
                act.wait_ge(s_job, n + 1)
                if what == "m":
                    nc.scalar.copy(maskT[:, b * HB:(b + 1) * HB, :], by_batch(bank)).then_inc(s_job_hi, 1)
                else:
                    dst = cT_hi if what == "c" else xT_hi
                    nc.scalar.copy(dst[:, :, b * SEQ:(b + 1) * SEQ], by_batch(bank)).then_inc(s_job_hi, 1)

            def whi(group, pos):
                act.wait_ge(s_raw[pos % 2], (group * 3 + pos // 2 + 1) * 16)
                wait_pos(act, s_proj, CHUNKS * (2 * group - 1) + pos + 1)
                nc.scalar.copy(W_hi[:, pos], W_raw[:, pos % 2]).then_inc(s_whi, 1)

            def wo_hi_part(group, h):
                act.wait_ge(s_wo_raw, group * 16 + 16)
                wait_pos(act, s_op, group * B)
                nc.scalar.copy(wo_hi[:, h, :], wo_raw[:, h, :]).then_inc(s_wo_hi, 1)

            def swap_halves(unit, pos, buf):
                r = unit * 5 + pos
                act.wait_ge(s_proj, unit * CHUNKS + pos + 1)
                wait_pos(act, s_roped, r - 1)
                rot_v = rot[:, (buf + pos) % 2, :]
                bank, H = ps[:, BANK_PROJ + pos % 2, :], DK // 2
                nc.scalar.copy(rot_v[0:H, :], bank[H:DK, :])
                nc.scalar.copy(rot_v[H:DK, :], bank[0:H, :]).then_inc(s_rot, 1)

            def khi(unit, buf):
                act.wait_ge(s_roped, unit * 5 + 1)
                wait_pos(act, s_scores, unit * HB - HB)
                nc.scalar.copy(K_hi[:, buf].rearrange("p b q -> p (b q)"), kvf[:, :]).then_inc(s_khi, 1)

            def vcopy(unit):
                act.wait_ge(s_proj, unit * CHUNKS + POS_V + 1)
                act.wait_ge(s_klo, unit + 1)
                nc.scalar.copy(kvf[:, :], ps[:, BANK_PROJ + POS_V % 2, :]).then_inc(s_vcopy, 1)

            def vhi(unit, buf):
                act.wait_ge(s_vt, unit + 1)
                wait_pos(act, s_pv, unit * HB - HB)
                nc.scalar.copy(V_hi[:, buf], by_batch(ps[:, BANK_VT, :])).then_inc(s_vhi, 1)

            def qhi(s, unit, k):
                act.wait_ge(s_roped, unit * 5 + 5)
                wait_pos(act, s_scores, s - 1)
                nc.scalar.copy(Q_hi[:, k % 2, :],
                               Qf[:, (k // HB) % 2, k % HB].rearrange("p h q -> p (h q)")).then_inc(s_qhi, 1)

            def ohi(s):
                act.wait_ge(s_on, s + 1)
                wait_pos(act, s_op, s)
                nc.scalar.copy(O_hi[:, :], nrec[:, :]).then_inc(s_ohi, 1)

            def probs(s, k):
                act.wait_ge(s_shift, s + 1)
                nc.scalar.activation(sc[:, k % 2, :], sc[:, k % 2, :], ACT.Exp).then_inc(s_exp, 1)
                act.wait_ge(s_exp, s + 1)
                wait_pos(act, s_pv, s - 1)
                nc.scalar.copy(P_hi[:, k % 2, :], sc[:, k % 2, :]).then_inc(s_phi, 1)

            def recip_seed(s):
                act.wait_ge(s_sum, s + 1)
                wait_pos(act, s_newton, s * 2)
                nc.scalar.activation(seed[:, :], ps[:, BANK_SUM, :], ACT.Ln).then_inc(s_ln, 1)
                act.wait_ge(s_ln, s + 1)
                nc.scalar.activation(seed[:, :], seed[:, :], ACT.Exp, scale=-1.0).then_inc(s_seed, 1)

            def tile(g, k, first=False, last=False):
                s = g * B + k
                nxt = g * 2 + k // HB + 1
                i = k % HB
                projecting = not (last and k >= HB)
                if not (first and k < 1):
                    probs(s - 1, k - 1)
                if not (first and k < 2):
                    ohi(s - 2)
                if k == 2:
                    for h in range(HPG):
                        wo_hi_part(g, h)
                if i == 0:
                    vhi(g * 2 + k // HB, k // HB)
                if i < 2:
                    qhi(s + 2, g * 2 + k // HB, k + 2)
                if projecting:
                    for pos in CHUNKS_AT[i]:
                        if pos != POS_V:
                            swap_halves(nxt, pos, (k // HB + 1) % 2)
                    if i == 1:
                        khi(nxt, (k // HB + 1) % 2)
                if i == HB - 1 and not (last and k == B - 1):
                    qhi(s + 1, nxt, k + 1)
                    qhi(s + 2, nxt, k + 2)
                if not (first and k < 1):
                    recip_seed(s - 1)
                if projecting and i == HB - 1:
                    vcopy(nxt)
                if not last:
                    for pos in CONVERT_AT.get(k, ()):
                        whi(g + 1, pos)

            act.wait_ge(s_chain, 2 * B + 1)
            nc.scalar.activation(sd[:, :], veps[:, :], ACT.Sqrt).then_inc(s_sqrt, 1)
            act.preload_act_table_set("natural_log_exp_and_others")
            act.wait_ge(s_ones_f, 1)
            nc.scalar.copy(ones[:, :], ones_f[:, :]).then_inc(s_ones, 1)
            for n in range(FIRST_JOBS):
                job(n)
                if n < CHUNKS:
                    whi(0, n)
            for pos in (0, 1):
                swap_halves(0, pos, 0)
            khi(0, 0)
            for pos in (2, 3, 4):
                swap_halves(0, pos, 0)
            vcopy(0)
            for n in range(FIRST_JOBS, ATT_JOBS):
                job(n)
            qhi(0, 0, 0)
            qhi(1, 0, 1)
            for k in range(B):
                tile(0, k, first=True)
            with act.Fori(1, GROUPS - 1) as g:
                for k in range(B):
                    tile(g, k)
            for k in range(B):
                tile(GROUPS - 1, k, last=True)
            probs(TILES - 1, B - 1)
            ohi(TILES - 2)
            recip_seed(TILES - 1)
            ohi(TILES - 1)

            act.wait_ge(s_chain, 2 * (2 * B + 1) + 4)
            nc.scalar.activation(sd[:, :], veps[:, :], ACT.Sqrt).then_inc(s_sqrt, 1)
            act.preload_act_table_set("silu_and_others")

            def fhi(t, m):
                act.wait_ge(s_fmul, t * NW + m + 1)
                if m < 4:
                    wait_pos(act, s_gu, t * 4 - 2 + 2 * (m // 2))
                else:
                    wait_pos(act, s_down, t * B)
                nc.scalar.copy(G_hi[:, m, :], F_w[:, m, :]).then_inc(s_fhi, 1)

            def silu(t, q):
                act.wait_ge(s_gu, t * 4 + q + 1)
                wait_pos(act, s_h, t * 4 + q)
                nc.scalar.activation(sg[:, :], ps[:, BANK_GATE + q % 2, :], ACT.Silu).then_inc(s_silu, 1)

            def hhi(t, q):
                i2, half = q // 2, q % 2
                act.wait_ge(s_h, t * 4 + q + 1)
                wait_pos(act, s_down, t * B - HB + half * HB)
                nc.scalar.copy(h_hi[:, i2, half * TOK:(half + 1) * TOK], hf[:, :]).then_inc(s_hhi, 1)

            def step(t, last=False):
                for q in range(4):
                    silu(t, q)
                    hhi(t, q)
                    if q == 0:
                        fhi(t, 2)
                        fhi(t, 3)
                    if q == 1:
                        fhi(t, 4)
                        fhi(t, 5)
                    if q == 2 and not last:
                        fhi(t + 1, 0)
                        fhi(t + 1, 1)

            for m in (0, 1):
                fhi(0, m)
            for n in range(ATT_JOBS, len(JOBS)):
                job(n)
            step(0)
            with act.Fori(1, FT - 1) as t:
                step(t)
            step(FT - 1, last=True)

        @block.vector
        def _(dve):
            chain = [0]

            def link(ins):
                chain[0] += 1
                ins.then_inc(s_chain, 1)

            def settle():
                dve.wait_ge(s_chain, chain[0])

            def statistics(second):
                for b in range(B):
                    if second:
                        if b == 0:
                            dve.wait_ge(s_acc, TILES)
                    else:
                        dve.wait_ge(s_x[b], 16)
                    link(nc.vector.bn_stats(bn[:, b, :], acc[:, b, :]))
                settle()
                for b in range(B):
                    link(nc.vector.bn_aggr(mv[:, b, :], bn[:, b, :]))
                settle()
                link(nc.vector.tensor_scalar(veps[:, :], mv[:, :, 1], EPS, None, ALU.add))

            def inverse_deviation(count):
                dve.wait_ge(s_sqrt, count)
                link(nc.vector.reciprocal(rstd[:, :], sd[:, :]))
                settle()
                link(nc.vector.tensor_tensor(nt[:, :], rstd[:, :], rstd[:, :], ALU.mult))
                settle()
                link(nc.vector.tensor_tensor(nt[:, :], nt[:, :], veps[:, :], ALU.mult))
                settle()
                link(nc.vector.tensor_scalar(nt[:, :], nt[:, :], -0.5, 1.5, ALU.mult, ALU.add))
                settle()
                nc.vector.tensor_tensor(rstd[:, :], rstd[:, :], nt[:, :], ALU.mult).then_inc(s_rstd, 1)
                dve.wait_ge(s_rstd, count)

            def normalise(n):
                b = JOBS[n][1]
                if staged_before(n) is not None:
                    dve.wait_ge(s_job, staged_before(n) + 1)
                nc.vector.tensor_scalar(stage_of(n), acc[:, b, :], mv[:, b, 0:1], rstd[:, b:b + 1],
                                        ALU.subtract, ALU.mult).then_inc(s_xn, 1)

            def job_lo(n):
                what, b = JOBS[n]
                if what == "m":
                    return
                hi, lo = (cT_hi, cT_lo) if what == "c" else (xT_hi, xT_lo)
                cols = slice(b * SEQ, (b + 1) * SEQ)
                dve.wait_ge(s_job_hi, n + 1)
                nc.vector.tensor_tensor(lo[:, :, cols], by_batch(ps[:, JOB_BANKS[n % 4], :]),
                                        hi[:, :, cols].bitcast(F32), ALU.subtract).then_inc(s_job_lo, 1)

            def rope(unit, pos, buf):
                r = unit * 5 + pos
                bank = by_batch(ps[:, BANK_PROJ + pos % 2, :])
                dst = by_batch(kvf[:, :]) if pos == POS_K else Qf[:, buf, :, HEAD_OF[pos], :]
                rot_v = by_batch(rot[:, (buf + pos) % 2, :])
                dve.wait_ge(s_rot, r + 1)
                if pos == POS_K:
                    wait_pos(dve, s_vt, unit)
                else:
                    wait_pos(dve, s_qlo, (unit - 1) * (HB - 1))
                nc.vector.tensor_tensor(dst, bank, cos_b, ALU.mult).then_inc(s_rope_cos, 1)
                nc.vector.tensor_tensor(rot_v, rot_v, sin_b, ALU.mult).then_inc(s_rope_sin, 1)
                dve.wait_ge(s_rope_cos, r + 1)
                dve.wait_ge(s_rope_sin, r + 1)
                nc.vector.tensor_tensor(dst, dst, rot_v, ALU.add).then_inc(s_roped, 1)

            def klo(unit, buf):
                dve.wait_ge(s_khi, unit + 1)
                nc.vector.tensor_tensor(K_lo[:, buf].rearrange("p b q -> p (b q)"), kvf[:, :],
                                        K_hi[:, buf].rearrange("p b q -> p (b q)").bitcast(F32),
                                        ALU.subtract).then_inc(s_klo, 1)

            def vlo(unit, buf):
                dve.wait_ge(s_vhi, unit + 1)
                nc.vector.tensor_tensor(V_lo[:, buf], by_batch(ps[:, BANK_VT, :]), V_hi[:, buf].bitcast(F32),
                                        ALU.subtract).then_inc(s_vlo, 1)

            def qlo_first(s, unit, k):
                dve.wait_ge(s_qhi, s + 1)
                nc.vector.tensor_tensor(Q_lo[:, k % 2, :],
                                        Qf[:, (k // HB) % 2, k % HB].rearrange("p h q -> p (h q)"),
                                        Q_hi[:, k % 2, :].bitcast(F32), ALU.subtract).then_inc(s_qlo_first, 1)

            def masked(s, k):
                dve.wait_ge(s_scores, s + 1)
                wait_pos(dve, s_plo, s - 1)
                nc.vector.scalar_tensor_tensor(
                    out=sc[:, k % 2, :].rearrange("p (h q) -> p h q", h=HPG),
                    in0=ps[:, BANK_SC + k % 2, :].rearrange("p (h q) -> p h q", h=HPG), scalar=SCALE,
                    in1=maskT[:, k, :].unsqueeze(1).broadcast_to([P, HPG, SEQ]),
                    op0=ALU.mult, op1=ALU.add).then_inc(s_masked, 1)

            def plo(s, k):
                dve.wait_ge(s_phi, s + 1)
                nc.vector.tensor_tensor(P_lo[:, k % 2, :], sc[:, k % 2, :], P_hi[:, k % 2, :].bitcast(F32),
                                        ALU.subtract).then_inc(s_plo, 1)

            def normalised_output(s):
                dve.wait_ge(s_seed, s + 1)
                wait_pos(dve, s_olo, s)
                nc.vector.tensor_tensor(nrec[:, :], ps[:, BANK_SUM, :], seed[:, :], ALU.mult).then_inc(s_newton, 1)
                dve.wait_ge(s_newton, s * 2 + 1)
                nc.vector.scalar_tensor_tensor(out=nrec[:, :], in0=nrec[:, :], scalar=-2.0, in1=seed[:, :],
                                               op0=ALU.add, op1=ALU.mult).then_inc(s_newton, 1)
                dve.wait_ge(s_newton, s * 2 + 2)
                dve.wait_ge(s_pv, s + 1)
                nc.vector.scalar_tensor_tensor(out=nrec[:, :], in0=ps[:, BANK_PV, :], scalar=-1.0, in1=nrec[:, :],
                                               op0=ALU.mult, op1=ALU.mult).then_inc(s_on, 1)

            def olo(s):
                dve.wait_ge(s_ohi, s + 1)
                nc.vector.tensor_tensor(O_lo[:, :], nrec[:, :], O_hi[:, :].bitcast(F32),
                                        ALU.subtract).then_inc(s_olo, 1)

            def add_attention(s, k):
                dve.wait_ge(s_op, s + 1)
                wait_pos(dve, s_acc, s - 3)
                nc.vector.tensor_tensor(acc[:, k, :], ps[:, BANK_OP, :], acc[:, k, :], ALU.add).then_inc(s_acc, 1)

            def wo_lo_part(group, h):
                dve.wait_ge(s_wo_hi, group * HPG + h + 1)
                nc.vector.tensor_tensor(wo_lo[:, h, :], wo_raw[:, h, :], wo_hi[:, h, :].bitcast(F32),
                                        ALU.subtract).then_inc(s_wo_lo, 1)

            def tile(g, k, first=False, last=False):
                s = g * B + k
                nxt = g * 2 + k // HB + 1
                i = k % HB
                projecting = not (last and k >= HB)
                masked(s, k)
                if not (first and k < 1):
                    plo(s - 1, k - 1)
                if not (first and k < 2):
                    olo(s - 2)
                if k == 2:
                    for h in range(HPG):
                        wo_lo_part(g, h)
                if not (first and k < 3):
                    add_attention(s - 3, (k - 3) % B)
                if i == 0:
                    vlo(g * 2 + k // HB, k // HB)
                if projecting:
                    for pos in CHUNKS_AT[i]:
                        if pos != POS_V:
                            rope(nxt, pos, (k // HB + 1) % 2)
                    if i == 1:
                        klo(nxt, (k // HB + 1) % 2)
                if i == HB - 1 and not (last and k == B - 1):
                    qlo_first(s + 1, nxt, k + 1)
                if not (first and k < 1):
                    normalised_output(s - 1)

            statistics(False)
            for n in range(HB):
                job_lo(n)
            inverse_deviation(1)
            for n in range(HB, FIRST_JOBS):
                if JOBS[n][0] == "x":
                    normalise(n)
            for n in range(HB, FIRST_JOBS):
                job_lo(n)
            dve.wait_ge(s_const, 32)
            rope(0, 0, 0)
            rope(0, 1, 0)
            klo(0, 0)
            for pos in (2, 3, 4):
                rope(0, pos, 0)
            for n in range(FIRST_JOBS, ATT_JOBS):
                if JOBS[n][0] == "c":
                    job_lo(n)
            for n in range(FIRST_JOBS, ATT_JOBS):
                if JOBS[n][0] == "x":
                    normalise(n)
            for n in range(FIRST_JOBS, ATT_JOBS):
                if JOBS[n][0] == "x":
                    job_lo(n)
            qlo_first(0, 0, 0)
            for k in range(B):
                tile(0, k, first=True)
            with dve.Fori(1, GROUPS - 1) as g:
                for k in range(B):
                    tile(g, k)
            for k in range(B):
                tile(GROUPS - 1, k, last=True)
            plo(TILES - 1, B - 1)
            olo(TILES - 2)
            add_attention(TILES - 3, B - 3)
            add_attention(TILES - 2, B - 2)
            normalised_output(TILES - 1)
            olo(TILES - 1)
            add_attention(TILES - 1, B - 1)

            def fsub(t, m):
                dve.wait_ge(s_fin[m], t * 48 + 48)
                nc.vector.tensor_tensor(F_w[:, m, :], F_w[:, m, :].bitcast(I32), F_z[:, m, :],
                                        ALU.subtract).then_inc(s_fsub, 1)

            def flo(t, m):
                dve.wait_ge(s_fhi, t * NW + m + 1)
                nc.vector.tensor_tensor(G_lo[:, m, :], F_w[:, m, :], G_hi[:, m, :].bitcast(F32),
                                        ALU.subtract).then_inc(s_flo, 1)

            def h_mul(t, q):
                dve.wait_ge(s_silu, t * 4 + q + 1)
                wait_pos(dve, s_hlo, t * 4 + q)
                nc.vector.tensor_tensor(hf[:, :], ps[:, BANK_UP + q % 2, :], sg[:, :], ALU.mult).then_inc(s_h, 1)

            def h_split(t, q):
                i2, cols = q // 2, slice((q % 2) * TOK, (q % 2 + 1) * TOK)
                dve.wait_ge(s_hhi, t * 4 + q + 1)
                nc.vector.tensor_tensor(h_lo[:, i2, cols], hf[:, :], h_hi[:, i2, cols].bitcast(F32),
                                        ALU.subtract).then_inc(s_hlo, 1)

            def add_ffn(t, half):
                for b in range(HB):
                    dve.wait_ge(s_down, t * B + half * HB + b + 1)
                    wait_pos(dve, s_facc, t * B + half * HB + b - 3)
                    nc.vector.tensor_tensor(acc[:, half * HB + b, :], ps[:, BANK_DOWN + b, :],
                                            acc[:, half * HB + b, :], ALU.add).then_inc(s_facc, 1)

            def step(t, first=False, last=False):
                fsub(t, 2)
                fsub(t, 3)
                h_mul(t, 0)
                h_split(t, 0)
                flo(t, 2)
                flo(t, 3)
                if not first:
                    add_ffn(t - 1, 1)
                fsub(t, 4)
                fsub(t, 5)
                h_mul(t, 1)
                h_split(t, 1)
                flo(t, 4)
                flo(t, 5)
                if not last:
                    fsub(t + 1, 0)
                    fsub(t + 1, 1)
                h_mul(t, 2)
                h_split(t, 2)
                if not last:
                    flo(t + 1, 0)
                    flo(t + 1, 1)
                h_mul(t, 3)
                h_split(t, 3)
                add_ffn(t, 0)

            statistics(True)
            fsub(0, 0)
            fsub(0, 1)
            inverse_deviation(2)
            for n in range(ATT_JOBS, ATT_JOBS + HB):
                normalise(n)
            for n in range(ATT_JOBS, ATT_JOBS + HB):
                job_lo(n)
            flo(0, 0)
            flo(0, 1)
            for n in range(ATT_JOBS + HB, len(JOBS)):
                normalise(n)
            for n in range(ATT_JOBS + HB, len(JOBS)):
                job_lo(n)
            step(0, first=True)
            with dve.Fori(1, FT - 1) as t:
                step(t)
            step(FT - 1, last=True)
            add_ffn(FT - 1, 1)

        @block.tensor
        def _(pe):
            def split_product(bank, terms):
                n = len(terms)
                for t, (l_hi, l_lo, r_hi, r_lo) in enumerate(terms):
                    nc.tensor.matmul(bank, l_lo, r_hi, start=(t == 0), stop=False)
                    nc.tensor.matmul(bank, l_hi, r_lo, start=False, stop=False)
                    last = nc.tensor.matmul(bank, l_hi, r_hi, start=False, stop=(t == n - 1))
                return last

            def job(n):
                what, b = JOBS[n]
                if what == "c":
                    pe.wait_ge(s_c[b % HB], 16 * (b // HB + 1))
                elif what == "m":
                    pe.wait_ge(s_m[b], 16)
                else:
                    pe.wait_ge(s_xn, normalised_before(n) + 1)
                if n >= 4:
                    pe.wait_ge(s_job_hi, n - 3)
                    pe.wait_ge(s_job_lo, lo_jobs(n - 3))
                src = mask_raw[b][:, :] if what == "m" else stage_of(n)
                for t in range(4):
                    last = nc.tensor.transpose(ps[:, JOB_BANKS[n % 4], t * P:(t + 1) * P],
                                               src[:, t * P:(t + 1) * P], ident[:, :])
                last.then_inc(s_job, 1)

            def project(unit, pos, half):
                pe.wait_ge(s_wlo, (unit - half) * (CHUNKS // 2) + pos + 1)
                before = pos - 2
                if before >= 0:
                    read_chunk_wait(pe, unit, before)
                elif not (isinstance(unit, int) and unit == 0):
                    read_chunk_wait(pe, unit - 1, before + CHUNKS)
                src_hi, src_lo = (cT_hi, cT_lo) if pos in (POS_K, POS_V) else (xT_hi, xT_lo)
                cols = slice(half * TOK, (half + 1) * TOK)
                split_product(ps[:, BANK_PROJ + pos % 2, :],
                              [(W_hi[:, pos, t, :], W_lo[:, pos, t, :], src_hi[:, t, cols], src_lo[:, t, cols])
                               for t in range(KT)]).then_inc(s_proj, 1)

            def transpose_v(unit):
                pe.wait_ge(s_vcopy, unit + 1)
                wait_pos(pe, s_vlo, unit)
                for b in range(HB):
                    last = nc.tensor.transpose(ps[:, BANK_VT, b * DK:(b + 1) * DK],
                                               kvf[:, b * SEQ:(b + 1) * SEQ], ident[:, :])
                last.then_inc(s_vt, 1)

            def scores(s, unit, k):
                buf = (k // HB) % 2
                if k % HB == 0:
                    pe.wait_ge(s_qlo_first, unit + 1)
                    pe.wait_ge(s_klo, unit + 1)
                else:
                    pe.wait_ge(s_qlo, unit * (HB - 1) + k % HB)
                wait_pos(pe, s_masked, s - 1)
                split_product(ps[:, BANK_SC + k % 2, :],
                              [(K_hi[:, buf, k % HB, :], K_lo[:, buf, k % HB, :],
                                Q_hi[:, k % 2, :], Q_lo[:, k % 2, :])]).then_inc(s_scores, 1)

            def sum_and_pv(s, unit, k):
                buf = (k // HB) % 2
                pe.wait_ge(s_plo, s + 1)
                wait_pos(pe, s_on, s)
                nc.tensor.matmul(ps[:, BANK_SUM, :], ones[:, :], P_lo[:, k % 2, :], start=True, stop=False)
                nc.tensor.matmul(ps[:, BANK_SUM, :], ones[:, :], P_hi[:, k % 2, :], start=False,
                                 stop=True).then_inc(s_sum, 1)
                if k % HB == 0:
                    pe.wait_ge(s_vlo, unit + 1)
                split_product(ps[:, BANK_PV, :],
                              [(V_hi[:, buf, k % HB, :], V_lo[:, buf, k % HB, :],
                                P_hi[:, k % 2, :], P_lo[:, k % 2, :])]).then_inc(s_pv, 1)

            def output_projection(s, group, k):
                pe.wait_ge(s_olo, s + 1)
                if k == 0:
                    pe.wait_ge(s_wo_lo, group * HPG + HPG)
                wait_pos(pe, s_acc, s)
                split_product(ps[:, BANK_OP, :],
                              [(O_hi[:, h * SEQ:(h + 1) * SEQ], O_lo[:, h * SEQ:(h + 1) * SEQ],
                                wo_hi[:, h, :], wo_lo[:, h, :]) for h in range(HPG)]).then_inc(s_op, 1)

            def tile(g, k, first=False, last=False):
                s = g * B + k
                nxt = g * 2 + k // HB + 1
                i = k % HB
                projecting = not (last and k >= HB)
                scores(s, g * 2 + k // HB, k)
                if i == 0:
                    transpose_v(g * 2 + k // HB)
                if projecting:
                    for pos in CHUNKS_AT[i]:
                        project(nxt, pos, (k // HB + 1) % 2)
                if not (first and k < 1):
                    sum_and_pv(s - 1, g * 2 + (k - 1) // HB, (k - 1) % B)
                if not (first and k < 2):
                    output_projection(s - 2, g if k >= 2 else g - 1, (k - 2) % B)

            pe.wait_ge(s_ident, 2)
            for n in range(FIRST_JOBS):
                job(n)
            pe.wait_ge(s_job_lo, lo_jobs(FIRST_JOBS))
            for pos in range(CHUNKS):
                project(0, pos, 0)
            for n in range(FIRST_JOBS, ATT_JOBS):
                job(n)
            pe.wait_ge(s_job_lo, lo_jobs(ATT_JOBS))
            pe.wait_ge(s_job_hi, ATT_JOBS)
            pe.wait_ge(s_ones, 1)
            for k in range(B):
                tile(0, k, first=True)
            with pe.Fori(1, GROUPS - 1) as g:
                for k in range(B):
                    tile(g, k)
            for k in range(B):
                tile(GROUPS - 1, k, last=True)
            sum_and_pv(TILES - 1, 2 * GROUPS - 1, B - 1)
            output_projection(TILES - 2, GROUPS - 1, B - 2)
            output_projection(TILES - 1, GROUPS - 1, B - 1)

            for n in range(ATT_JOBS, len(JOBS)):
                job(n)
            pe.wait_ge(s_job_lo, lo_jobs(len(JOBS)))

            def gate_up(t, q):
                i2, half = q // 2, q % 2
                pe.wait_ge(s_flo, t * NW + 2 * i2 + 2)
                wait_pos(pe, s_h, t * 4 + q - 1)
                cols = slice(half * TOK, (half + 1) * TOK)
                for m, bank in ((2 * i2, BANK_GATE), (2 * i2 + 1, BANK_UP)):
                    last = split_product(ps[:, bank + q % 2, :],
                                         [(G_hi[:, m, k * P:(k + 1) * P], G_lo[:, m, k * P:(k + 1) * P],
                                           xT_hi[:, k, cols], xT_lo[:, k, cols]) for k in range(KT)])
                last.then_inc(s_gu, 1)

            def down(t, half):
                pe.wait_ge(s_flo, t * NW + NW)
                pe.wait_ge(s_hlo, t * 4 + 3 + half)
                for b in range(HB):
                    wait_pos(pe, s_facc, t * B + half * HB + b - 3)
                    rows = slice(half * TOK + b * SEQ, half * TOK + (b + 1) * SEQ)
                    split_product(ps[:, BANK_DOWN + b, :],
                                  [(h_hi[:, i2, rows], h_lo[:, i2, rows], G_hi[:, 4 + i2, :], G_lo[:, 4 + i2, :])
                                   for i2 in range(2)]).then_inc(s_down, 1)

            def step(t, first=False):
                gate_up(t, 0)
                if not first:
                    down(t - 1, 1)
                gate_up(t, 1)
                gate_up(t, 2)
                gate_up(t, 3)
                down(t, 0)

            step(0, first=True)
            with pe.Fori(1, FT) as t:
                step(t)
            down(FT - 1, 1)


_INS = ["x", "ctx_4096", "mask_BxSxS2_ff0", "L0_xattn_wq", "L0_xattn_wk", "L0_xattn_wv", "L0_xattn_wo",
        "L0_ffn_gate_w", "L0_ffn_gate_z", "L0_ffn_gate_s", "L0_ffn_up_w", "L0_ffn_up_z", "L0_ffn_up_s",
        "L0_ffn_down_w", "L0_ffn_down_z", "L0_ffn_down_s"]


def rope_tables():
    inv = (np.float32(1.0) / np.float32(ROPE_BASE) ** (np.arange(0, DK, 2, dtype=np.float32) / np.float32(DK)))
    ang = inv[:, None] * np.arange(SEQ, dtype=np.float32)[None, :]
    cos, sin = np.cos(ang), np.sin(ang)
    return (np.ascontiguousarray(np.concatenate([cos, cos], 0), np.float32),
            np.ascontiguousarray(np.concatenate([-sin, sin], 0), np.float32))


def kernel(**inputs):
    import concourse.bacc as _bacc
    from concourse.bass_utils import run_bass_kernel_spmd as _run

    nc = _bacc.Bacc("TRN2", target_bir_lowering=False, num_devices=1)
    arrays, args = {}, []
    for name in _INS:
        arr = np.ascontiguousarray(inputs[name])
        arrays[f"in_{name}"] = arr
        args.append(nc.dram_tensor(f"in_{name}", arr.shape, mybir.dt.from_np(arr.dtype), kind="ExternalInput").ap())
    for name, arr in zip(("cos", "sin"), rope_tables()):
        arrays[f"in_{name}"] = arr
        args.append(nc.dram_tensor(f"in_{name}", arr.shape, F32, kind="ExternalInput").ap())
    args.append(nc.dram_tensor("out_0", (B, SEQ, DM), F32, kind="ExternalOutput").ap())
    build(nc, *args)
    r = _run(nc, [arrays], core_ids=[0])
    return r.results[0]["out_0"]
```

```python
from contextlib import ExitStack

import numpy as np

import concourse.bass as bass
from concourse import mybir

F32 = mybir.dt.float32
F32R = mybir.dt.float32r
I32 = mybir.dt.int32
ALU = mybir.AluOpType
ACT = mybir.ActivationFunctionType
RMAX = bass.bass_isa.ReduceOp.max

P = 128
B = 8
SEQ = 128
DM = 512
KT = DM // P
DK = 128
GROUPS = 8
HPG = 4
HB = B // 2
TOK = HB * SEQ
TILES = GROUPS * B
FF = 1792
FT = FF // (2 * P)
NW = 6
EPS = 1e-5
ROPE_BASE = 10000.0
SCALE = float(DK) ** -0.5

CHUNKS = 6
POS_K, POS_V = 0, 5
HEAD_OF = {1: 0, 2: 1, 3: 2, 4: 3}
CHUNKS_AT = ((0, 1), (2, 3), (4,), (5,))
CONVERT_AT = {2: (0, 1), 3: (2,), 4: (3, 4), 5: (5,)}
HEADS_POOL, HEADS_DVE = (0, 1), (2, 3)
FIRST_FINAL = TILES - B


def wait_pos(e, sem, value):
    if isinstance(value, int) and value <= 0:
        return
    e.wait_ge(sem, value)


def build(nc, x, ctx, mask, wq, wk, wv, wo, gate_w, gate_z, gate_s, up_w, up_z, up_s,
          down_w, down_z, down_s, cos_in, sin_in, out):
    with ExitStack() as top:
        def sb(stack, name, shape, dt=F32):
            return stack.enter_context(nc.sbuf_tensor(name, shape, dt))

        def sem(name):
            return top.enter_context(nc.semaphore(name))

        acc = sb(top, "acc", [P, B, DM])
        xT_hi = sb(top, "xT_hi", [P, KT, B * SEQ], F32R)
        xT_lo = sb(top, "xT_lo", [P, KT, B * SEQ], F32R)
        Qf = sb(top, "Qf", [P, 2, HB, HPG, SEQ])
        stage = Qf[:, 1].rearrange("p b h q -> p b (h q)")
        cosT = sb(top, "cosT", [P, SEQ])
        sinT = sb(top, "sinT", [P, SEQ])
        ident = sb(top, "ident", [P, P])
        ones = sb(top, "ones", [P, P], F32R)
        ones_f = sb(top, "ones_f", [P, P])
        bn = sb(top, "bn", [P, B, 6])
        mv = sb(top, "mv", [P, B, 2])
        veps = sb(top, "veps", [P, B])
        lnv = sb(top, "lnv", [P, B])
        rstd = sb(top, "rstd", [P, B])
        nmr = sb(top, "nmr", [P, B])
        nt = sb(top, "nt", [P, B])

        with ExitStack() as a:
            cT_hi = sb(a, "cT_hi", [P, KT, B * SEQ], F32R)
            cT_lo = sb(a, "cT_lo", [P, KT, B * SEQ], F32R)
            W_hi = sb(a, "W_hi", [P, CHUNKS, KT, DK], F32R)
            W_lo = sb(a, "W_lo", [P, CHUNKS, KT, DK], F32R)
            W_raw = sb(a, "W_raw", [P, 2, KT, DK])
            wo_raw = sb(a, "wo_raw", [P, HPG, DM])
            rot = sb(a, "rot", [P, 2, TOK])
            kvf = sb(a, "kvf", [P, TOK])
            K_hi = sb(a, "K_hi", [P, 2, HB, SEQ], F32R)
            K_lo = sb(a, "K_lo", [P, 2, HB, SEQ], F32R)
            wo_hi = sb(a, "wo_hi", [P, HPG, DM], F32R)
            wo_lo = sb(a, "wo_lo", [P, HPG, DM], F32R)
            Q_hi = sb(a, "Q_hi", [P, 2, HPG * SEQ], F32R)
            Q_lo = sb(a, "Q_lo", [P, 2, HPG * SEQ], F32R)
            V_hi = sb(a, "V_hi", [P, 2, HB, DK], F32R)
            V_lo = sb(a, "V_lo", [P, 2, HB, DK], F32R)
            maskT = sb(a, "maskT", [P, B, SEQ])
            sc = sb(a, "sc", [P, 2, HPG * SEQ])
            smax = sb(a, "smax", [P, HPG * SEQ])
            P_hi = sb(a, "P_hi", [P, 2, HPG * SEQ], F32R)
            P_lo = sb(a, "P_lo", [P, 2, HPG * SEQ], F32R)
            seed = sb(a, "seed", [P, HPG * SEQ])
            nrec = sb(a, "nrec", [P, HPG * SEQ])
            O_hi = sb(a, "O_hi", [P, HPG * SEQ], F32R)
            O_lo = sb(a, "O_lo", [P, HPG * SEQ], F32R)
        mask_raw = (seed, nrec)

        with ExitStack() as f:
            F_w = sb(f, "F_w", [P, NW, DM])
            F_z = sb(f, "F_z", [P, NW, DM], I32)
            F_s = sb(f, "F_s", [P, NW, DM])
            G_hi = sb(f, "G_hi", [P, NW, DM], F32R)
            G_lo = sb(f, "G_lo", [P, NW, DM], F32R)
            sg = sb(f, "sg", [P, TOK])
            hf = sb(f, "hf", [P, TOK])
            h_hi = sb(f, "h_hi", [P, 2, B * SEQ], F32R)
            h_lo = sb(f, "h_lo", [P, 2, B * SEQ], F32R)

        ps = top.enter_context(nc.psum_tensor("ps", [P, 8, 512], F32))
        BANK_PROJ, BANK_SC, BANK_PV, BANK_SUM, BANK_OP, BANK_VT = 0, 2, 4, 5, 6, 7
        BANK_GATE, BANK_UP, BANK_DOWN = 0, 2, 4

        s_const, s_ident, s_ones_f, s_ones = sem("s_const"), sem("s_ident"), sem("s_ones_f"), sem("s_ones")
        s_var, s_lnv, s_rseed, s_rstd = sem("s_var"), sem("s_lnv"), sem("s_rseed"), sem("s_rstd")
        s_x = [sem(f"s_x{b}") for b in range(B)]
        s_c = [sem(f"s_c{b}") for b in range(HB)]
        s_m = [sem(f"s_m{b}") for b in range(2)]
        s_chain, s_xn = sem("s_chain"), sem("s_xn")
        s_job, s_job_hi, s_job_lo = sem("s_job"), sem("s_job_hi"), sem("s_job_lo")
        s_raw = [sem("s_raw0"), sem("s_raw1")]
        s_whi, s_wlo = sem("s_whi"), sem("s_wlo")
        s_wo_raw, s_wo_hi = sem("s_wo_raw"), sem("s_wo_hi")
        s_wo_lo, s_wo_lo_pool = sem("s_wo_lo"), sem("s_wo_lo_pool")
        s_proj, s_rot, s_roped = sem("s_proj"), sem("s_rot"), sem("s_roped")
        s_rope_cos, s_rope_sin = sem("s_rope_cos"), sem("s_rope_sin")
        s_khi, s_klo = sem("s_khi"), sem("s_klo")
        s_vcopy, s_vt, s_vhi, s_vlo = sem("s_vcopy"), sem("s_vt"), sem("s_vhi"), sem("s_vlo")
        s_qhi, s_qlo, s_qlo_first = sem("s_qhi"), sem("s_qlo"), sem("s_qlo_first")
        s_scores, s_masked, s_max_go = sem("s_scores"), sem("s_masked"), sem("s_max_go")
        s_max, s_shift = sem("s_max"), sem("s_shift")
        s_exp, s_phi, s_plo = sem("s_exp"), sem("s_phi"), sem("s_plo")
        s_sum, s_pv, s_ln, s_seed = sem("s_sum"), sem("s_pv"), sem("s_ln"), sem("s_seed")
        s_newton, s_on, s_ohi, s_olo = sem("s_newton"), sem("s_on"), sem("s_ohi"), sem("s_olo")
        s_op, s_acc = sem("s_op"), sem("s_acc")
        s_fin = [sem(f"s_fin{m}") for m in range(NW)]
        s_fsub, s_fmul, s_fhi, s_flo = sem("s_fsub"), sem("s_fmul"), sem("s_fhi"), sem("s_flo")
        s_gu, s_silu, s_h, s_hhi, s_hlo = sem("s_gu"), sem("s_silu"), sem("s_h"), sem("s_hhi"), sem("s_hlo")
        s_down, s_facc, s_out = sem("s_down"), sem("s_facc"), sem("s_out")

        JOBS = [("c", b) for b in range(HB)] + [("x", b) for b in range(HB)] + [("m", 0)]
        FIRST_JOBS = len(JOBS)
        JOBS += [("c", b) for b in range(HB, B)] + [("x", b) for b in range(HB, B)] + [("m", 1)]
        SECOND_X = FIRST_JOBS + HB
        ATT_JOBS = len(JOBS)
        JOBS += [("y", b) for b in range(B)]

        def lo_jobs(n):
            return sum(what != "m" for what, _ in JOBS[:n])

        JOB_BANK = [2, 3, 4, 5] * 3 + [2] + [3, 4, 5, 6, 1] + [0, 1, 7, 3] + [4, 5, 7, 6]

        def bank_before(n):
            first = 0 if n < ATT_JOBS else ATT_JOBS
            same = [m for m in range(first, n) if JOB_BANK[m] == JOB_BANK[n]]
            return same[-1] if same else None

        def stage_of(n):
            what, b = JOBS[n]
            if what == "y":
                return Qf[:, b // HB, b % HB].rearrange("p h q -> p (h q)")
            return stage[:, b % HB, :]

        def staged_before(n):
            same = [m for m in range(n) if JOBS[m][0] != "m" and JOBS[m][1] % HB == JOBS[n][1] % HB]
            return same[-1] if same and JOBS[n][0] != "y" else None

        def normalised_before(n):
            return sum(what in "xy" for what, _ in JOBS[:n])

        wq_v = wq.rearrange("(t p) n -> p t n", p=P)
        wk_v = wk.rearrange("(t p) n -> p t n", p=P)
        wv_v = wv.rearrange("(t p) n -> p t n", p=P)
        wo_v = wo.rearrange("(h p) n -> p h n", p=DK)
        gate_v = gate_w.rearrange("(t p) n -> p t n", p=P)
        up_v = up_w.rearrange("(t p) n -> p t n", p=P)

        cos_b = cosT[:, :].unsqueeze(1).broadcast_to([P, HB, SEQ])

        sin_b = sinT[:, :].unsqueeze(1).broadcast_to([P, HB, SEQ])

        def by_batch(ap):
            return ap.rearrange("p (b q) -> p b q", b=HB)

        def read_chunk_wait(e, c_unit, pos):
            if pos == POS_V:
                wait_pos(e, s_vcopy, c_unit + 1)
            else:
                wait_pos(e, s_rope_cos, 5 * c_unit + pos + 1)

        block = top.enter_context(nc.Block())

        @block.sync
        def _(sp):
            def load_piece(group, pos):
                wait_pos(sp, s_wlo, CHUNKS * group + pos - 1)
                if pos == POS_K:
                    src = wk_v[:, :, bass.ds(group * DK, DK)]
                elif pos == POS_V:
                    src = wv_v[:, :, bass.ds(group * DK, DK)]
                else:
                    src = wq_v[:, :, bass.ds((group * HPG + HEAD_OF[pos]) * DK, DK)]
                sp.dma_start(W_raw[:, pos % 2], src).then_inc(s_raw[pos % 2], 16)

            def load_wo(group):
                wait_pos(sp, s_wo_lo, len(HEADS_DVE) * group)
                wait_pos(sp, s_wo_lo_pool, len(HEADS_POOL) * group)
                sp.dma_start(wo_raw[:, :, :], wo_v[:, bass.ds(group * HPG, HPG), :]).then_inc(s_wo_raw, 16)

            for b in range(HB):
                sp.dma_start(acc[:, b, :], x[b]).then_inc(s_x[b], 16)
                sp.dma_start(stage[:, b, :], ctx[b]).then_inc(s_c[b], 16)
            load_piece(0, 0)
            sp.dma_start(cosT[:, :], cos_in).then_inc(s_const, 16)
            sp.dma_start(sinT[:, :], sin_in).then_inc(s_const, 16)
            for pos in (1, 2):
                load_piece(0, pos)
            for b in range(HB, B):
                sp.dma_start(acc[:, b, :], x[b]).then_inc(s_x[b], 16)
            for half in range(2):
                sp.dma_start(mask_raw[half][:, :].rearrange("p (b k) -> p b k", b=HB),
                             mask[half * HB:(half + 1) * HB].rearrange("b q k -> q b k")).then_inc(s_m[half], 16)
            load_piece(0, 3)
            for n in range(FIRST_JOBS, SECOND_X):
                sp.wait_ge(s_job, staged_before(n) + 1)
                sp.dma_start(stage_of(n), ctx[JOBS[n][1]]).then_inc(s_c[JOBS[n][1] - HB], 16)
            for pos in (4, 5):
                load_piece(0, pos)
            load_wo(0)

            with sp.Fori(0, GROUPS - 1) as g:
                for pos in range(CHUNKS):
                    load_piece(g + 1, pos)
                load_wo(g + 1)

            def load_ffn(t, m):
                if m < 4:
                    w_v, z, s = (gate_v, gate_z, gate_s) if m % 2 == 0 else (up_v, up_z, up_s)
                    col = t * (2 * P) + (m // 2) * P
                    sp.dma_start(F_w[:, m, :].bitcast(I32).rearrange("p (t n) -> p t n", t=KT),
                                 w_v[:, :, bass.ds(col, P)]).then_inc(s_fin[m], 16)
                    for dst, src in ((F_z, z), (F_s, s)):
                        sp.dma_start(dst[:, m, :].rearrange("p (t n) -> p t n", t=KT),
                                     src[:, bass.ds(col, P)].partition_broadcast(P)).then_inc(s_fin[m], 16)
                else:
                    row = t * (2 * P) + (m - 4) * P
                    sp.dma_start(F_w[:, m, :].bitcast(I32), down_w[bass.ds(row, P), :]).then_inc(s_fin[m], 16)
                    for dst, src in ((F_z, down_z), (F_s, down_s)):
                        sp.dma_start(dst[:, m:m + 1, :],
                                     src[bass.ds(t * 2 + (m - 4), 1), :].partition_broadcast(P)).then_inc(s_fin[m], 16)

            sp.wait_ge(s_proj, CHUNKS * 2 * GROUPS)
            for m in range(NW):
                load_ffn(0, m)
            with sp.Fori(0, FT - 1) as t:
                for m in range(NW):
                    sp.wait_ge(s_flo, t * NW + m + 1)
                    load_ffn(t + 1, m)
            for half in range(2):
                for b in range(HB):
                    sp.wait_ge(s_facc, B * (FT - 1) + half * HB + b + 1)
                    sp.dma_start(out[half * HB + b], acc[:, half * HB + b, :]).then_inc(s_out, 16)
            sp.wait_ge(s_out, 16 * B)

        @block.gpsimd
        def _(pool):
            nc.gpsimd.memset(ones_f[:, :], 1.0).then_inc(s_ones_f, 1)
            nc.gpsimd.memset(ident[:, :], 0.0).then_inc(s_ident, 1)
            pool.wait_ge(s_ident, 1)
            nc.gpsimd.affine_select(out=ident[:, :], in_=ident[:, :], compare_op=ALU.not_equal, fill=1.0,
                                    base=0, pattern=[[-1, P]], channel_multiplier=1).then_inc(s_ident, 1)

            def split_piece(group, pos):
                pool.wait_ge(s_whi, group * CHUNKS + pos + 1)
                nc.gpsimd.tensor_tensor(W_lo[:, pos], W_raw[:, pos % 2], W_hi[:, pos].bitcast(F32),
                                        ALU.subtract).then_inc(s_wlo, 1)

            def qlo(s, k):
                pool.wait_ge(s_qhi, s + 1)
                nc.gpsimd.tensor_tensor(Q_lo[:, k % 2, :],
                                        Qf[:, (k // HB) % 2, k % HB].rearrange("p h q -> p (h q)"),
                                        Q_hi[:, k % 2, :].bitcast(F32), ALU.subtract).then_inc(s_qlo, 1)

            def tile(g, k, last=False):
                s = g * B + k
                pool.wait_ge(s_masked, s + 1)
                wait_pos(pool, s_shift, s)
                pool.sem_inc(s_max_go, 1)
                nc.gpsimd.partition_all_reduce(smax[:, :], sc[:, k % 2, :], P, RMAX).then_inc(s_max, 1)
                pool.wait_ge(s_max, s + 1)
                nc.gpsimd.tensor_tensor(sc[:, k % 2, :], sc[:, k % 2, :], smax[:, :],
                                        ALU.subtract).then_inc(s_shift, 1)
                if k % HB < 2:
                    qlo(s + 2, k + 2)
                elif k % HB == HB - 1 and not (last and k == B - 1):
                    qlo(s + 2, k + 2)
                if k == 1:
                    for h in HEADS_POOL:
                        pool.wait_ge(s_wo_hi, g * HPG + h + 1)
                        nc.gpsimd.tensor_tensor(wo_lo[:, h, :], wo_raw[:, h, :], wo_hi[:, h, :].bitcast(F32),
                                                ALU.subtract).then_inc(s_wo_lo_pool, 1)
                if not last:
                    for pos in CONVERT_AT.get(k, ()):
                        split_piece(g + 1, pos)

            for pos in range(CHUNKS):
                split_piece(0, pos)
            qlo(1, 1)
            with pool.Fori(0, GROUPS - 1) as g:
                for k in range(B):
                    tile(g, k)
            for k in range(B):
                tile(GROUPS - 1, k, last=True)

            def scale_piece(t, m):
                pool.wait_ge(s_fsub, t * NW + m + 1)
                nc.gpsimd.tensor_tensor(F_w[:, m, :], F_w[:, m, :], F_s[:, m, :], ALU.mult).then_inc(s_fmul, 1)

            with pool.Fori(0, FT - 1) as t:
                for m in (2, 3, 4, 5):
                    scale_piece(t, m)
                for m in (0, 1):
                    scale_piece(t + 1, m)
            for m in (2, 3, 4, 5):
                scale_piece(FT - 1, m)

        @block.scalar
        def _(act):
            def job(n):
                what, b = JOBS[n]
                bank = ps[:, JOB_BANK[n], :]
                act.wait_ge(s_job, n + 1)
                if what == "m":
                    nc.scalar.copy(maskT[:, b * HB:(b + 1) * HB, :], by_batch(bank)).then_inc(s_job_hi, 1)
                else:
                    dst = cT_hi if what == "c" else xT_hi
                    nc.scalar.copy(dst[:, :, b * SEQ:(b + 1) * SEQ], by_batch(bank)).then_inc(s_job_hi, 1)

            def whi(group, pos):
                act.wait_ge(s_raw[pos % 2], (group * 3 + pos // 2 + 1) * 16)
                wait_pos(act, s_proj, CHUNKS * (2 * group - 1) + pos + 1)
                nc.scalar.copy(W_hi[:, pos], W_raw[:, pos % 2]).then_inc(s_whi, 1)

            def wo_hi_part(group, h):
                act.wait_ge(s_wo_raw, group * 16 + 16)
                wait_pos(act, s_op, group * B)
                nc.scalar.copy(wo_hi[:, h, :], wo_raw[:, h, :]).then_inc(s_wo_hi, 1)

            def swap_halves(unit, pos, buf):
                r = unit * 5 + pos
                act.wait_ge(s_proj, unit * CHUNKS + pos + 1)
                wait_pos(act, s_roped, r - 1)
                rot_v = rot[:, (buf + pos) % 2, :]
                bank, H = ps[:, BANK_PROJ + pos % 2, :], DK // 2
                nc.scalar.copy(rot_v[0:H, :], bank[H:DK, :])
                nc.scalar.copy(rot_v[H:DK, :], bank[0:H, :]).then_inc(s_rot, 1)

            def khi(unit, buf):
                act.wait_ge(s_roped, unit * 5 + 1)
                wait_pos(act, s_scores, unit * HB - HB)
                nc.scalar.copy(K_hi[:, buf].rearrange("p b q -> p (b q)"), kvf[:, :]).then_inc(s_khi, 1)

            def vcopy(unit):
                act.wait_ge(s_proj, unit * CHUNKS + POS_V + 1)
                act.wait_ge(s_klo, unit + 1)
                nc.scalar.copy(kvf[:, :], ps[:, BANK_PROJ + POS_V % 2, :]).then_inc(s_vcopy, 1)

            def vhi(unit, buf):
                act.wait_ge(s_vt, unit + 1)
                wait_pos(act, s_pv, unit * HB - HB)
                nc.scalar.copy(V_hi[:, buf], by_batch(ps[:, BANK_VT, :])).then_inc(s_vhi, 1)

            def qhi(s, unit, k):
                act.wait_ge(s_roped, unit * 5 + 5)
                wait_pos(act, s_scores, s - 1)
                nc.scalar.copy(Q_hi[:, k % 2, :],
                               Qf[:, (k // HB) % 2, k % HB].rearrange("p h q -> p (h q)")).then_inc(s_qhi, 1)

            def ohi(s):
                act.wait_ge(s_on, s + 1)
                wait_pos(act, s_op, s)
                nc.scalar.copy(O_hi[:, :], nrec[:, :]).then_inc(s_ohi, 1)

            def probs(s, k):
                act.wait_ge(s_shift, s + 1)
                nc.scalar.activation(sc[:, k % 2, :], sc[:, k % 2, :], ACT.Exp).then_inc(s_exp, 1)
                act.wait_ge(s_exp, s + 1)
                wait_pos(act, s_pv, s - 1)
                nc.scalar.copy(P_hi[:, k % 2, :], sc[:, k % 2, :]).then_inc(s_phi, 1)

            def recip_seed(s):
                act.wait_ge(s_sum, s + 1)
                wait_pos(act, s_newton, s * 2)
                nc.scalar.activation(seed[:, :], ps[:, BANK_SUM, :], ACT.Ln).then_inc(s_ln, 1)
                act.wait_ge(s_ln, s + 1)
                nc.scalar.activation(seed[:, :], seed[:, :], ACT.Exp, scale=-1.0).then_inc(s_seed, 1)

            def inverse_deviation_seed(m):
                cols = slice((m % 2) * HB, (m % 2 + 1) * HB)
                act.wait_ge(s_var, m + 1)
                nc.scalar.activation(lnv[:, cols], veps[:, cols], ACT.Ln).then_inc(s_lnv, 1)
                act.wait_ge(s_lnv, m + 1)
                nc.scalar.activation(rstd[:, cols], lnv[:, cols], ACT.Exp, scale=-0.5).then_inc(s_rseed, 1)

            def normalise(n):
                what, b = JOBS[n]
                norm_half = b // HB + (2 if what == "y" else 0)
                act.wait_ge(s_rstd, norm_half + 1)
                if what == "x":
                    act.wait_ge(s_job, staged_before(n) + 1)
                else:
                    act.wait_ge(s_qlo, (2 * GROUPS - 1 + b // HB) * (HB - 1))
                nc.scalar.activation(stage_of(n), acc[:, b, :], ACT.Identity, bias=nmr[:, b:b + 1],
                                     scale=rstd[:, b:b + 1]).then_inc(s_xn, 1)

            def fhi(t, m):
                act.wait_ge(s_fmul, t * NW + m + 1)
                if m < 4:
                    wait_pos(act, s_gu, t * 4 - 1 + m // 2)
                else:
                    wait_pos(act, s_down, t * B)
                nc.scalar.copy(G_hi[:, m, :], F_w[:, m, :]).then_inc(s_fhi, 1)

            def tile(g, k, first=False, last=False):
                s = g * B + k
                nxt = g * 2 + k // HB + 1
                i = k % HB
                projecting = not (last and k >= HB)
                if not (first and k < 1):
                    probs(s - 1, k - 1)
                if not (first and k < 2):
                    ohi(s - 2)
                if k == 2:
                    for h in HEADS_DVE:
                        wo_hi_part(g, h)
                if i == 0:
                    vhi(g * 2 + k // HB, k // HB)
                if i < 2:
                    qhi(s + 2, g * 2 + k // HB, k + 2)
                if projecting:
                    for pos in CHUNKS_AT[i]:
                        if pos != POS_V:
                            swap_halves(nxt, pos, (k // HB + 1) % 2)
                    if i == 1:
                        khi(nxt, (k // HB + 1) % 2)
                if i == HB - 1 and not (last and k == B - 1):
                    qhi(s + 1, nxt, k + 1)
                    qhi(s + 2, nxt, k + 2)
                if not (first and k < 1):
                    recip_seed(s - 1)
                if k == 1:
                    for h in HEADS_POOL:
                        wo_hi_part(g, h)
                if projecting and i == HB - 1:
                    vcopy(nxt)
                if not last:
                    for pos in CONVERT_AT.get(k, ()):
                        whi(g + 1, pos)

            act.preload_act_table_set("natural_log_exp_and_others")
            act.wait_ge(s_ones_f, 1)
            nc.scalar.copy(ones[:, :], ones_f[:, :]).then_inc(s_ones, 1)
            for n in range(HB):
                job(n)
                if n == 1:
                    inverse_deviation_seed(0)
            for n in range(HB, 2 * HB):
                normalise(n)
            whi(0, 0)
            for n in range(HB, 2 * HB):
                job(n)
            whi(0, 1)
            whi(0, 2)
            swap_halves(0, POS_K, 0)
            job(2 * HB)
            whi(0, 3)
            khi(0, 0)
            for pos in (1, 2, 3, 4):
                swap_halves(0, pos, 0)
                job(FIRST_JOBS + pos - 1)
                if pos + 3 < CHUNKS:
                    whi(0, pos + 3)
                if pos == 3:
                    inverse_deviation_seed(1)
                if pos == 4:
                    for n in range(SECOND_X, SECOND_X + HB):
                        normalise(n)
            vcopy(0)
            qhi(0, 0, 0)
            qhi(1, 0, 1)
            for n in range(SECOND_X, ATT_JOBS):
                job(n)
            for k in range(B):
                tile(0, k, first=True)
            with act.Fori(1, GROUPS - 1) as g:
                for k in range(B):
                    tile(g, k)
            for k in range(B):
                tile(GROUPS - 1, k, last=True)
            inverse_deviation_seed(2)
            fhi(0, 0)
            fhi(0, 1)
            probs(TILES - 1, B - 1)
            ohi(TILES - 2)
            for n in range(ATT_JOBS, ATT_JOBS + HB):
                normalise(n)
            recip_seed(TILES - 1)
            job(ATT_JOBS)
            job(ATT_JOBS + 1)
            ohi(TILES - 1)
            job(ATT_JOBS + 2)
            job(ATT_JOBS + 3)
            fhi(0, 2)
            fhi(0, 3)
            inverse_deviation_seed(3)
            act.preload_act_table_set("silu_and_others")
            for n in range(ATT_JOBS + HB, len(JOBS)):
                normalise(n)

            def silu(t, q):
                act.wait_ge(s_gu, t * 4 + q + 1)
                wait_pos(act, s_h, t * 4 + q)
                nc.scalar.activation(sg[:, :], ps[:, BANK_GATE + q % 2, :], ACT.Silu).then_inc(s_silu, 1)

            def hhi(t, q):
                half, i2 = q // 2, q % 2
                act.wait_ge(s_h, t * 4 + q + 1)
                wait_pos(act, s_down, t * B - HB + half * HB)
                nc.scalar.copy(h_hi[:, i2, half * TOK:(half + 1) * TOK], hf[:, :]).then_inc(s_hhi, 1)

            def step(t, first=False, last=False):
                for q in range(4):
                    silu(t, q)
                    hhi(t, q)
                    if q == 0 and not first:
                        fhi(t, 2)
                        fhi(t, 3)
                    if q == 0 and first:
                        for n in range(ATT_JOBS + HB, len(JOBS)):
                            job(n)
                    if q == 1:
                        fhi(t, 4)
                        fhi(t, 5)
                    if q == 2 and not last:
                        fhi(t + 1, 0)
                        fhi(t + 1, 1)

            step(0, first=True)
            with act.Fori(1, FT - 1) as t:
                step(t)
            step(FT - 1, last=True)

        @block.vector
        def _(dve):
            chain = [0]

            def link(ins):
                chain[0] += 1
                ins.then_inc(s_chain, 1)

            def settle():
                dve.wait_ge(s_chain, chain[0])

            def statistics(b, second=True):
                if second:
                    dve.wait_ge(s_acc, FIRST_FINAL + b + 1)
                else:
                    dve.wait_ge(s_x[b], 16)
                link(nc.vector.bn_stats(bn[:, b, :], acc[:, b, :]))
                settle()
                link(nc.vector.bn_aggr(mv[:, b, :], bn[:, b, :]))

            def variance(m):
                cols = slice((m % 2) * HB, (m % 2 + 1) * HB)
                settle()
                nc.vector.tensor_scalar(veps[:, cols], mv[:, cols, 1], EPS, None, ALU.add).then_inc(s_var, 1)

            def inverse_deviation(m):
                cols = slice((m % 2) * HB, (m % 2 + 1) * HB)
                dve.wait_ge(s_rseed, m + 1)
                link(nc.vector.tensor_tensor(nt[:, cols], rstd[:, cols], rstd[:, cols], ALU.mult))
                settle()
                link(nc.vector.tensor_tensor(nt[:, cols], nt[:, cols], veps[:, cols], ALU.mult))
                settle()
                link(nc.vector.tensor_scalar(nt[:, cols], nt[:, cols], -0.5, 1.5, ALU.mult, ALU.add))
                settle()
                link(nc.vector.tensor_tensor(rstd[:, cols], rstd[:, cols], nt[:, cols], ALU.mult))
                settle()
                nc.vector.scalar_tensor_tensor(out=nmr[:, cols], in0=mv[:, cols, 0], scalar=-1.0, in1=rstd[:, cols],
                                               op0=ALU.mult, op1=ALU.mult).then_inc(s_rstd, 1)

            def job_lo(n):
                what, b = JOBS[n]
                if what == "m":
                    return
                hi, lo = (cT_hi, cT_lo) if what == "c" else (xT_hi, xT_lo)
                cols = slice(b * SEQ, (b + 1) * SEQ)
                dve.wait_ge(s_job_hi, n + 1)
                nc.vector.tensor_tensor(lo[:, :, cols], by_batch(ps[:, JOB_BANK[n], :]),
                                        hi[:, :, cols].bitcast(F32), ALU.subtract).then_inc(s_job_lo, 1)

            def rope(unit, pos, buf):
                r = unit * 5 + pos
                bank = by_batch(ps[:, BANK_PROJ + pos % 2, :])
                dst = by_batch(kvf[:, :]) if pos == POS_K else Qf[:, buf, :, HEAD_OF[pos], :]
                rot_v = by_batch(rot[:, (buf + pos) % 2, :])
                dve.wait_ge(s_rot, r + 1)
                if pos == POS_K:
                    wait_pos(dve, s_vt, unit)
                else:
                    wait_pos(dve, s_qlo, (unit - 1) * (HB - 1))
                nc.vector.tensor_tensor(dst, bank, cos_b, ALU.mult).then_inc(s_rope_cos, 1)
                nc.vector.tensor_tensor(rot_v, rot_v, sin_b, ALU.mult).then_inc(s_rope_sin, 1)
                dve.wait_ge(s_rope_cos, r + 1)
                dve.wait_ge(s_rope_sin, r + 1)
                nc.vector.tensor_tensor(dst, dst, rot_v, ALU.add).then_inc(s_roped, 1)

            def klo(unit, buf):
                dve.wait_ge(s_khi, unit + 1)
                nc.vector.tensor_tensor(K_lo[:, buf].rearrange("p b q -> p (b q)"), kvf[:, :],
                                        K_hi[:, buf].rearrange("p b q -> p (b q)").bitcast(F32),
                                        ALU.subtract).then_inc(s_klo, 1)

            def vlo(unit, buf):
                dve.wait_ge(s_vhi, unit + 1)
                nc.vector.tensor_tensor(V_lo[:, buf], by_batch(ps[:, BANK_VT, :]), V_hi[:, buf].bitcast(F32),
                                        ALU.subtract).then_inc(s_vlo, 1)

            def qlo_first(s, unit, k):
                dve.wait_ge(s_qhi, s + 1)
                nc.vector.tensor_tensor(Q_lo[:, k % 2, :],
                                        Qf[:, (k // HB) % 2, k % HB].rearrange("p h q -> p (h q)"),
                                        Q_hi[:, k % 2, :].bitcast(F32), ALU.subtract).then_inc(s_qlo_first, 1)

            def masked(s, k):
                dve.wait_ge(s_scores, s + 1)
                wait_pos(dve, s_plo, s - 1)
                nc.vector.scalar_tensor_tensor(
                    out=sc[:, k % 2, :].rearrange("p (h q) -> p h q", h=HPG),
                    in0=ps[:, BANK_SC + k % 2, :].rearrange("p (h q) -> p h q", h=HPG), scalar=SCALE,
                    in1=maskT[:, k, :].unsqueeze(1).broadcast_to([P, HPG, SEQ]),
                    op0=ALU.mult, op1=ALU.add).then_inc(s_masked, 1)

            def plo(s, k):
                dve.wait_ge(s_phi, s + 1)
                nc.vector.tensor_tensor(P_lo[:, k % 2, :], sc[:, k % 2, :], P_hi[:, k % 2, :].bitcast(F32),
                                        ALU.subtract).then_inc(s_plo, 1)

            def normalised_output(s):
                dve.wait_ge(s_seed, s + 1)
                wait_pos(dve, s_olo, s)
                nc.vector.tensor_tensor(nrec[:, :], ps[:, BANK_SUM, :], seed[:, :], ALU.mult).then_inc(s_newton, 1)
                dve.wait_ge(s_newton, s * 2 + 1)
                nc.vector.scalar_tensor_tensor(out=nrec[:, :], in0=nrec[:, :], scalar=-2.0, in1=seed[:, :],
                                               op0=ALU.add, op1=ALU.mult).then_inc(s_newton, 1)
                dve.wait_ge(s_newton, s * 2 + 2)
                dve.wait_ge(s_pv, s + 1)
                nc.vector.scalar_tensor_tensor(out=nrec[:, :], in0=ps[:, BANK_PV, :], scalar=-1.0, in1=nrec[:, :],
                                               op0=ALU.mult, op1=ALU.mult).then_inc(s_on, 1)

            def olo(s):
                dve.wait_ge(s_ohi, s + 1)
                nc.vector.tensor_tensor(O_lo[:, :], nrec[:, :], O_hi[:, :].bitcast(F32),
                                        ALU.subtract).then_inc(s_olo, 1)

            def add_attention(s, k):
                dve.wait_ge(s_op, s + 1)
                wait_pos(dve, s_acc, s - 3)
                nc.vector.tensor_tensor(acc[:, k, :], ps[:, BANK_OP, :], acc[:, k, :], ALU.add).then_inc(s_acc, 1)

            def wo_lo_part(group, h):
                dve.wait_ge(s_wo_hi, group * HPG + h + 1)
                nc.vector.tensor_tensor(wo_lo[:, h, :], wo_raw[:, h, :], wo_hi[:, h, :].bitcast(F32),
                                        ALU.subtract).then_inc(s_wo_lo, 1)

            def fsub(t, m):
                dve.wait_ge(s_fin[m], t * 48 + 48)
                nc.vector.tensor_tensor(F_w[:, m, :], F_w[:, m, :].bitcast(I32), F_z[:, m, :],
                                        ALU.subtract).then_inc(s_fsub, 1)

            def flo(t, m):
                dve.wait_ge(s_fhi, t * NW + m + 1)
                nc.vector.tensor_tensor(G_lo[:, m, :], F_w[:, m, :], G_hi[:, m, :].bitcast(F32),
                                        ALU.subtract).then_inc(s_flo, 1)

            def fscale(m):
                dve.wait_ge(s_fsub, m + 1)
                nc.vector.tensor_tensor(F_w[:, m, :], F_w[:, m, :], F_s[:, m, :], ALU.mult).then_inc(s_fmul, 1)

            def tile(g, k, first=False, last=False):
                s = g * B + k
                nxt = g * 2 + k // HB + 1
                i = k % HB
                projecting = not (last and k >= HB)
                masked(s, k)
                if first and k == 0:
                    for n in range(SECOND_X, SECOND_X + HB):
                        job_lo(n)
                if not (first and k < 1):
                    plo(s - 1, k - 1)
                if not (first and k < 2):
                    olo(s - 2)
                if not (first and k < 3):
                    add_attention(s - 3, (k - 3) % B)
                    if last and k >= 3:
                        statistics(k - 3)
                if k == 2:
                    for h in HEADS_DVE:
                        wo_lo_part(g, h)
                if i == 0:
                    vlo(g * 2 + k // HB, k // HB)
                if projecting:
                    for pos in CHUNKS_AT[i]:
                        if pos != POS_V:
                            rope(nxt, pos, (k // HB + 1) % 2)
                    if i == 3:
                        klo(nxt, (k // HB + 1) % 2)
                if i == HB - 1 and not (last and k == B - 1):
                    qlo_first(s + 1, nxt, k + 1)
                if last and k == 5:
                    fsub(0, 0)
                if last and k == 6:
                    variance(2)
                    fscale(0)
                    fsub(0, 1)
                if last and k == 7:
                    fscale(1)
                if not (first and k < 1):
                    normalised_output(s - 1)

            for b in range(HB):
                statistics(b, second=False)
            variance(0)
            job_lo(0)
            job_lo(1)
            inverse_deviation(0)
            for n in range(2, 2 * HB):
                job_lo(n)
            dve.wait_ge(s_const, 32)
            rope(0, 0, 0)
            klo(0, 0)
            statistics(4, second=False)
            for pos in (1, 2, 3, 4):
                rope(0, pos, 0)
                job_lo(FIRST_JOBS + pos - 1)
                if pos == 1:
                    statistics(5, second=False)
                if pos == 2:
                    statistics(6, second=False)
                    statistics(7, second=False)
                    variance(1)
                if pos == 3:
                    inverse_deviation(1)
            qlo_first(0, 0, 0)
            for k in range(B):
                tile(0, k, first=True)
            with dve.Fori(1, GROUPS - 1) as g:
                for k in range(B):
                    tile(g, k)
            for k in range(B):
                tile(GROUPS - 1, k, last=True)
            inverse_deviation(2)
            plo(TILES - 1, B - 1)
            olo(TILES - 2)
            add_attention(TILES - 3, B - 3)
            fsub(0, 2)
            fsub(0, 3)
            statistics(B - 3)
            normalised_output(TILES - 1)
            add_attention(TILES - 2, B - 2)
            job_lo(ATT_JOBS)
            job_lo(ATT_JOBS + 1)
            olo(TILES - 1)
            job_lo(ATT_JOBS + 2)
            job_lo(ATT_JOBS + 3)
            flo(0, 0)
            flo(0, 1)
            statistics(B - 2)
            add_attention(TILES - 1, B - 1)
            flo(0, 2)
            statistics(B - 1)
            variance(3)
            flo(0, 3)
            inverse_deviation(3)

            def h_mul(t, q):
                dve.wait_ge(s_silu, t * 4 + q + 1)
                wait_pos(dve, s_hlo, t * 4 + q)
                nc.vector.tensor_tensor(hf[:, :], ps[:, BANK_UP + q % 2, :], sg[:, :], ALU.mult).then_inc(s_h, 1)

            def h_split(t, q):
                i2, cols = q % 2, slice((q // 2) * TOK, (q // 2 + 1) * TOK)
                dve.wait_ge(s_hhi, t * 4 + q + 1)
                nc.vector.tensor_tensor(h_lo[:, i2, cols], hf[:, :], h_hi[:, i2, cols].bitcast(F32),
                                        ALU.subtract).then_inc(s_hlo, 1)

            def add_ffn(t, half):
                for b in range(HB):
                    dve.wait_ge(s_down, t * B + half * HB + b + 1)
                    wait_pos(dve, s_facc, t * B + half * HB + b - 3)
                    nc.vector.tensor_tensor(acc[:, half * HB + b, :], ps[:, BANK_DOWN + b, :],
                                            acc[:, half * HB + b, :], ALU.add).then_inc(s_facc, 1)

            def step(t, first=False, last=False):
                if not first:
                    fsub(t, 2)
                    fsub(t, 3)
                h_mul(t, 0)
                h_split(t, 0)
                if first:
                    for n in range(ATT_JOBS + HB, len(JOBS)):
                        job_lo(n)
                else:
                    flo(t, 2)
                    flo(t, 3)
                fsub(t, 4)
                fsub(t, 5)
                if not first:
                    add_ffn(t - 1, 1)
                h_mul(t, 1)
                h_split(t, 1)
                flo(t, 4)
                flo(t, 5)
                if not last:
                    fsub(t + 1, 0)
                    fsub(t + 1, 1)
                h_mul(t, 2)
                h_split(t, 2)
                if not last:
                    flo(t + 1, 0)
                    flo(t + 1, 1)
                if not last:
                    add_ffn(t, 0)
                h_mul(t, 3)
                h_split(t, 3)
                if last:
                    add_ffn(t, 0)

            step(0, first=True)
            with dve.Fori(1, FT - 1) as t:
                step(t)
            step(FT - 1, last=True)
            add_ffn(FT - 1, 1)

        @block.tensor
        def _(pe):
            def split_product(bank, terms, start=True, stop=True):
                n = len(terms)
                for t, (l_hi, l_lo, r_hi, r_lo) in enumerate(terms):
                    nc.tensor.matmul(bank, l_lo, r_hi, start=(start and t == 0), stop=False)
                    nc.tensor.matmul(bank, l_hi, r_lo, start=False, stop=False)
                    last = nc.tensor.matmul(bank, l_hi, r_hi, start=False, stop=(stop and t == n - 1))
                return last

            def job(n):
                what, b = JOBS[n]
                if what == "c":
                    pe.wait_ge(s_c[b % HB], 16 * (b // HB + 1))
                elif what == "m":
                    pe.wait_ge(s_m[b], 16)
                else:
                    pe.wait_ge(s_xn, normalised_before(n) + 1)
                if bank_before(n) is not None:
                    pe.wait_ge(s_job_hi, bank_before(n) + 1)
                    pe.wait_ge(s_job_lo, lo_jobs(bank_before(n) + 1))
                src = mask_raw[b][:, :] if what == "m" else stage_of(n)
                for t in range(4):
                    last = nc.tensor.transpose(ps[:, JOB_BANK[n], t * P:(t + 1) * P],
                                               src[:, t * P:(t + 1) * P], ident[:, :])
                last.then_inc(s_job, 1)

            def project(unit, pos, half):
                pe.wait_ge(s_wlo, (unit - half) * (CHUNKS // 2) + pos + 1)
                before = pos - 2
                if before >= 0:
                    read_chunk_wait(pe, unit, before)
                elif not (isinstance(unit, int) and unit == 0):
                    read_chunk_wait(pe, unit - 1, before + CHUNKS)
                src_hi, src_lo = (cT_hi, cT_lo) if pos in (POS_K, POS_V) else (xT_hi, xT_lo)
                cols = slice(half * TOK, (half + 1) * TOK)
                split_product(ps[:, BANK_PROJ + pos % 2, :],
                              [(W_hi[:, pos, t, :], W_lo[:, pos, t, :], src_hi[:, t, cols], src_lo[:, t, cols])
                               for t in range(KT)]).then_inc(s_proj, 1)

            def transpose_v(unit):
                pe.wait_ge(s_vcopy, unit + 1)
                wait_pos(pe, s_vlo, unit)
                for b in range(HB):
                    last = nc.tensor.transpose(ps[:, BANK_VT, b * DK:(b + 1) * DK],
                                               kvf[:, b * SEQ:(b + 1) * SEQ], ident[:, :])
                last.then_inc(s_vt, 1)

            def scores(s, unit, k):
                buf = (k // HB) % 2
                if k % HB == 0:
                    pe.wait_ge(s_qlo_first, unit + 1)
                    pe.wait_ge(s_klo, unit + 1)
                else:
                    pe.wait_ge(s_qlo, unit * (HB - 1) + k % HB)
                wait_pos(pe, s_masked, s - 1)
                split_product(ps[:, BANK_SC + k % 2, :],
                              [(K_hi[:, buf, k % HB, :], K_lo[:, buf, k % HB, :],
                                Q_hi[:, k % 2, :], Q_lo[:, k % 2, :])]).then_inc(s_scores, 1)

            def sum_and_pv(s, unit, k):
                buf = (k // HB) % 2
                pe.wait_ge(s_plo, s + 1)
                wait_pos(pe, s_on, s)
                nc.tensor.matmul(ps[:, BANK_SUM, :], ones[:, :], P_lo[:, k % 2, :], start=True, stop=False)
                nc.tensor.matmul(ps[:, BANK_SUM, :], ones[:, :], P_hi[:, k % 2, :], start=False,
                                 stop=True).then_inc(s_sum, 1)
                if k % HB == 0:
                    pe.wait_ge(s_vlo, unit + 1)
                split_product(ps[:, BANK_PV, :],
                              [(V_hi[:, buf, k % HB, :], V_lo[:, buf, k % HB, :],
                                P_hi[:, k % 2, :], P_lo[:, k % 2, :])]).then_inc(s_pv, 1)

            def output_projection(s, group, k):
                pe.wait_ge(s_olo, s + 1)
                wait_pos(pe, s_acc, s)
                for h in range(HPG):
                    if k == 0:
                        if h in HEADS_POOL:
                            pe.wait_ge(s_wo_lo_pool, group * len(HEADS_POOL) + h + 1)
                        else:
                            pe.wait_ge(s_wo_lo, group * len(HEADS_DVE) + h - len(HEADS_POOL) + 1)
                    O_h, O_l = O_hi[:, h * SEQ:(h + 1) * SEQ], O_lo[:, h * SEQ:(h + 1) * SEQ]
                    last = split_product(ps[:, BANK_OP, :], [(O_h, O_l, wo_hi[:, h, :], wo_lo[:, h, :])],
                                         start=(h == 0), stop=(h == HPG - 1))
                last.then_inc(s_op, 1)

            def tile(g, k, first=False, last=False):
                s = g * B + k
                nxt = g * 2 + k // HB + 1
                i = k % HB
                projecting = not (last and k >= HB)
                scores(s, g * 2 + k // HB, k)
                if i == 0:
                    transpose_v(g * 2 + k // HB)
                if projecting:
                    for pos in CHUNKS_AT[i]:
                        project(nxt, pos, (k // HB + 1) % 2)
                        if first and k == 0 and pos == POS_K:
                            pe.wait_ge(s_job_hi, ATT_JOBS)
                            pe.wait_ge(s_job_lo, lo_jobs(ATT_JOBS))
                if not (first and k < 1):
                    sum_and_pv(s - 1, g * 2 + (k - 1) // HB, (k - 1) % B)
                if not (first and k < 2):
                    output_projection(s - 2, g if k >= 2 else g - 1, (k - 2) % B)

            pe.wait_ge(s_ident, 2)
            for n in range(HB):
                job(n)
            for n in range(HB, 2 * HB):
                job(n)
            pe.wait_ge(s_job_lo, HB)
            project(0, POS_K, 0)
            pe.wait_ge(s_job_lo, 2 * HB)
            project(0, 1, 0)
            job(2 * HB)
            for pos in range(2, CHUNKS):
                job(FIRST_JOBS + pos - 2)
                project(0, pos, 0)
            for n in range(SECOND_X, SECOND_X + HB):
                job(n)
            pe.wait_ge(s_vcopy, 1)
            job(ATT_JOBS - 1)
            pe.wait_ge(s_job_hi, SECOND_X)
            pe.wait_ge(s_job_lo, lo_jobs(SECOND_X))
            pe.wait_ge(s_ones, 1)
            for k in range(B):
                tile(0, k, first=True)
            with pe.Fori(1, GROUPS - 1) as g:
                for k in range(B):
                    tile(g, k)
            for k in range(B):
                tile(GROUPS - 1, k, last=True)
            def gate_up(t, q):
                half, i2 = q // 2, q % 2
                pe.wait_ge(s_flo, t * NW + 2 * i2 + 2)
                wait_pos(pe, s_h, t * 4 + q - 1)
                cols = slice(half * TOK, (half + 1) * TOK)
                for m, bank in ((2 * i2, BANK_GATE), (2 * i2 + 1, BANK_UP)):
                    last = split_product(ps[:, bank + q % 2, :],
                                         [(G_hi[:, m, k * P:(k + 1) * P], G_lo[:, m, k * P:(k + 1) * P],
                                           xT_hi[:, k, cols], xT_lo[:, k, cols]) for k in range(KT)])
                last.then_inc(s_gu, 1)

            def down(t, half):
                pe.wait_ge(s_flo, t * NW + NW)
                pe.wait_ge(s_hlo, t * 4 + 2 * half + 2)
                for b in range(HB):
                    wait_pos(pe, s_facc, t * B + half * HB + b - 3)
                    rows = slice(half * TOK + b * SEQ, half * TOK + (b + 1) * SEQ)
                    split_product(ps[:, BANK_DOWN + b, :],
                                  [(h_hi[:, i2, rows], h_lo[:, i2, rows], G_hi[:, 4 + i2, :], G_lo[:, 4 + i2, :])
                                   for i2 in range(2)]).then_inc(s_down, 1)

            sum_and_pv(TILES - 1, 2 * GROUPS - 1, B - 1)
            output_projection(TILES - 2, GROUPS - 1, B - 2)
            for n in range(ATT_JOBS, ATT_JOBS + HB):
                job(n)
            output_projection(TILES - 1, GROUPS - 1, B - 1)
            pe.wait_ge(s_job_lo, lo_jobs(ATT_JOBS + HB))
            gate_up(0, 0)
            gate_up(0, 1)
            for n in range(ATT_JOBS + HB, len(JOBS)):
                job(n)
            pe.wait_ge(s_job_lo, lo_jobs(len(JOBS)))

            def step(t, first=False, last=False):
                if not first:
                    gate_up(t, 0)
                    down(t - 1, 1)
                    gate_up(t, 1)
                gate_up(t, 2)
                if last:
                    gate_up(t, 3)
                    down(t, 0)
                    down(t, 1)
                else:
                    down(t, 0)
                    gate_up(t, 3)

            step(0, first=True)
            with pe.Fori(1, FT - 1) as t:
                step(t)
            step(FT - 1, last=True)


_INS = ["x", "ctx_4096", "mask_BxSxS2_ff0", "L0_xattn_wq", "L0_xattn_wk", "L0_xattn_wv", "L0_xattn_wo",
        "L0_ffn_gate_w", "L0_ffn_gate_z", "L0_ffn_gate_s", "L0_ffn_up_w", "L0_ffn_up_z", "L0_ffn_up_s",
        "L0_ffn_down_w", "L0_ffn_down_z", "L0_ffn_down_s"]


def rope_tables():
    inv = (np.float32(1.0) / np.float32(ROPE_BASE) ** (np.arange(0, DK, 2, dtype=np.float32) / np.float32(DK)))
    ang = inv[:, None] * np.arange(SEQ, dtype=np.float32)[None, :]
    cos, sin = np.cos(ang), np.sin(ang)
    return (np.ascontiguousarray(np.concatenate([cos, cos], 0), np.float32),
            np.ascontiguousarray(np.concatenate([-sin, sin], 0), np.float32))


def kernel(**inputs):
    import concourse.bacc as _bacc
    from concourse.bass_utils import run_bass_kernel_spmd as _run

    nc = _bacc.Bacc("TRN2", target_bir_lowering=False, num_devices=1)
    arrays, args = {}, []
    for name in _INS:
        arr = np.ascontiguousarray(inputs[name])
        arrays[f"in_{name}"] = arr
        args.append(nc.dram_tensor(f"in_{name}", arr.shape, mybir.dt.from_np(arr.dtype), kind="ExternalInput").ap())
    for name, arr in zip(("cos", "sin"), rope_tables()):
        arrays[f"in_{name}"] = arr
        args.append(nc.dram_tensor(f"in_{name}", arr.shape, F32, kind="ExternalInput").ap())
    args.append(nc.dram_tensor("out_0", (B, SEQ, DM), F32, kind="ExternalOutput").ap())
    build(nc, *args)
    r = _run(nc, [arrays], core_ids=[0])
    return r.results[0]["out_0"]
```
